# Optimizing a Trainium2 kernel written in Bass

```python
import numpy as np
import jax
import jax.numpy as jnp

def _softmax(x, axis=-1):
    return jax.nn.softmax(x, axis=axis)

def _gelu(x):
    return jax.nn.gelu(x, approximate=True)

def _silu(x):
    return jax.nn.silu(x)

def _sigmoid(x):
    return jax.nn.sigmoid(x)

def _layernorm(x, axis=-1, eps=1e-05):
    m = jnp.mean(x, axis=axis, keepdims=True)
    v = jnp.var(x, axis=axis, keepdims=True)
    return (x - m) / jnp.sqrt(v + eps)

def _scatter_add(tgt, idx, src, axis=0):
    return tgt.at[idx].add(src)

def _segment_sum(src, seg, n):
    return jax.ops.segment_sum(src, seg, n)
kernel_name = 'mk_seq_preln_d1_jaxref_r8_61cbba'

def setup_inputs(seed: int=0):
    np.random.seed(seed)
    _w = jnp.asarray

    def _L0_attn_setup():
        import jax, jax.numpy as jnp
        import numpy as np
        B, S, D = (4, 256, 128)
        H, K = (16, 64)
        EPS = 0.001
        key = jax.random.key(seed)
        ks = jax.random.split(key, 11)
        s = 0.02
        return {'x': jax.random.normal(ks[0], (B, S, D), jnp.float32), 'Wq': jax.random.normal(ks[1], (D, H, K), jnp.float32) * s, 'bq': jnp.zeros((H, K), jnp.float32), 'Wk': jax.random.normal(ks[2], (D, H, K), jnp.float32) * s, 'bk': jnp.zeros((H, K), jnp.float32), 'Wv': jax.random.normal(ks[3], (D, H, K), jnp.float32) * s, 'bv': jnp.zeros((H, K), jnp.float32), 'Wo': jax.random.normal(ks[4], (H, K, D), jnp.float32) * s, 'bo': jnp.zeros((D,), jnp.float32), 'gamma': jnp.ones((D,), jnp.float32), 'beta': jnp.zeros((D,), jnp.float32)}
    _L0_attn_in = _L0_attn_setup()

    def _L0_ffn_setup():
        import jax, jax.numpy as jnp
        import numpy as np
        B, S, D = (4, 256, 128)
        EXP = 4
        H = EXP * D
        E = 8
        TOP_K = 2
        key = jax.random.key(seed)
        ks = jax.random.split(key, 8)
        scale1 = 1.0 / np.sqrt(D)
        scale2 = 1.0 / np.sqrt(H)
        x = jax.random.normal(ks[0], (B, S, D), dtype=jnp.float32)
        W1 = jax.random.uniform(ks[1], (E, D, H), jnp.float32, -scale1, scale1)
        b1 = jax.random.uniform(ks[2], (E, H), jnp.float32, -scale1, scale1)
        W2 = jax.random.uniform(ks[3], (E, H, D), jnp.float32, -scale2, scale2)
        b2 = jax.random.uniform(ks[4], (E, D), jnp.float32, -scale2, scale2)
        Wr = jax.random.uniform(ks[5], (D, E), jnp.float32, -scale1, scale1)
        br = jax.random.uniform(ks[6], (E,), jnp.float32, -scale1, scale1)
        return {'input_emb': x, 'W1': W1, 'b1': b1, 'W2': W2, 'b2': b2, 'Wr': Wr, 'br': br}
    _L0_ffn_in = _L0_ffn_setup()
    _d = {'L0_attn_x': _L0_attn_in['x'], 'L0_attn_Wq': _L0_attn_in['Wq'], 'L0_attn_bq': _L0_attn_in['bq'], 'L0_attn_Wk': _L0_attn_in['Wk'], 'L0_attn_bk': _L0_attn_in['bk'], 'L0_attn_Wv': _L0_attn_in['Wv'], 'L0_attn_bv': _L0_attn_in['bv'], 'L0_attn_Wo': _L0_attn_in['Wo'], 'L0_attn_bo': _L0_attn_in['bo'], 'L0_attn_gamma': _L0_attn_in['gamma'], 'L0_attn_beta': _L0_attn_in['beta'], 'L0_ffn_W1': _L0_ffn_in['W1'], 'L0_ffn_b1': _L0_ffn_in['b1'], 'L0_ffn_W2': _L0_ffn_in['W2'], 'L0_ffn_b2': _L0_ffn_in['b2'], 'L0_ffn_Wr': _L0_ffn_in['Wr'], 'L0_ffn_br': _L0_ffn_in['br']}
    _x0 = _d['L0_attn_x']
    _d['L0_attn_x'] = jax.random.normal(jax.random.fold_in(jax.random.key(seed), 1), (4, 1024, 128), dtype=_x0.dtype)
    del _x0
    return _d

def reference(L0_attn_x, L0_attn_Wq, L0_attn_bq, L0_attn_Wk, L0_attn_bk, L0_attn_Wv, L0_attn_bv, L0_attn_Wo, L0_attn_bo, L0_attn_gamma, L0_attn_beta, L0_ffn_W1, L0_ffn_b1, L0_ffn_W2, L0_ffn_b2, L0_ffn_Wr, L0_ffn_br):

    def _L0_attn_ref(x, Wq, bq, Wk, bk, Wv, bv, Wo, bo, gamma, beta):
        import jax, jax.numpy as jnp
        import numpy as np
        B, S, D = (4, 256, 128)
        H, K = (16, 64)
        EPS = 0.001
        q = jnp.einsum('bsd,dhk->bshk', x, Wq) + bq
        k = jnp.einsum('bsd,dhk->bshk', x, Wk) + bk
        v = jnp.einsum('bsd,dhk->bshk', x, Wv) + bv
        scale = 1.0 / jnp.sqrt(jnp.asarray(K, x.dtype))
        scores = jnp.einsum('bqhk,bshk->bhqs', q, k) * scale
        attn = jax.nn.softmax(scores, axis=-1)
        ctx = jnp.einsum('bhqs,bshk->bqhk', attn, v)
        attn_out = jnp.einsum('bqhk,hkd->bqd', ctx, Wo) + bo
        y = x + attn_out
        mu = jnp.mean(y, axis=-1, keepdims=True)
        var = jnp.mean(jnp.square(y - mu), axis=-1, keepdims=True)
        return (y - mu) * jax.lax.rsqrt(var + EPS) * gamma + beta

    def _L0_ffn_ref(input_emb, W1, b1, W2, b2, Wr, br):
        import jax, jax.numpy as jnp
        import numpy as np
        B, S, D = (4, 256, 128)
        EXP = 4
        H = EXP * D
        E = 8
        TOP_K = 2
        logits = jnp.einsum('bsd,de->bse', input_emb, Wr) + br
        route_w = jax.nn.softmax(logits, axis=-1)
        _, topk_idx = jax.lax.top_k(route_w, TOP_K)
        mask = jax.nn.one_hot(topk_idx, E, dtype=route_w.dtype).sum(-2)
        routed = route_w * mask
        routed = routed / routed.sum(axis=-1, keepdims=True)
        h = jax.nn.relu(jnp.einsum('bsd,edh->ebsh', input_emb, W1) + b1[:, None, None, :])
        expert_out = jnp.einsum('ebsh,ehd->ebsd', h, W2) + b2[:, None, None, :]
        return jnp.einsum('bse,ebsd->bsd', routed, expert_out)
    x = L0_attn_x
    x = x + _L0_attn_ref(_layernorm(x, axis=-1), L0_attn_Wq, L0_attn_bq, L0_attn_Wk, L0_attn_bk, L0_attn_Wv, L0_attn_bv, L0_attn_Wo, L0_attn_bo, L0_attn_gamma, L0_attn_beta)
    x = x + _L0_ffn_ref(_layernorm(x, axis=-1), L0_ffn_W1, L0_ffn_b1, L0_ffn_W2, L0_ffn_b2, L0_ffn_Wr, L0_ffn_br)
    return x

_drawn_inputs = setup_inputs


def setup_inputs(seed=0):
    import zlib

    import numpy as np

    out = dict(_drawn_inputs(seed))
    spreads = {'L0_attn_bq': (0.0, 0.8),
     'L0_attn_bk': (0.0, 0.8),
     'L0_attn_bv': (0.0, 0.1),
     'L0_attn_bo': (0.0, 0.1),
     'L0_attn_gamma': (1.0, 0.2),
     'L0_attn_beta': (0.0, 0.1)}
    factors = {'L0_attn_Wq': 8.0,
     'L0_attn_Wk': 8.0,
     'L0_attn_Wv': 8.0,
     'L0_ffn_b1': 7.641,
     'L0_ffn_b2': 6.454}
    for name, (base, spread) in spreads.items():
        noise = np.random.default_rng([zlib.crc32(name.encode()), seed]).standard_normal(out[name].shape)
        drawn = base * np.exp(spread * noise) if base else spread * noise
        out[name] = jnp.asarray(drawn.astype(out[name].dtype))
    for name, factor in factors.items():
        out[name] = (out[name] * factor).astype(out[name].dtype)
    return out
```

```python
from contextlib import ExitStack

import concourse.bass as bass
from concourse import mybir

ALU = mybir.AluOpType
ACT = mybir.ActivationFunctionType
AX = mybir.AxisListType
F32 = mybir.dt.float32
F16 = mybir.dt.float16
BF16 = mybir.dt.bfloat16

P = 128


def block_kernel(nc, x, Wq, bq, Wk, bk, Wv, bv, Wo, bo, gamma, beta, W1, b1, W2, b2, Wr, br, out):
    B, S, D = x.shape
    H, K = Wq.shape[1:]
    E, _, F = W1.shape
    assert D == P and 2 * K == P and S % 512 == 0
    ATTN_EPS, LN_EPS = 1e-3, 1e-5
    SCALE = K ** -0.5
    HEADROOM = 8.0
    TILES = B * S // P
    PAIRS_PER_BATCH = H // 2
    PAIRS = B * PAIRS_PER_BATCH
    KT = S // P
    HK = H * K
    GROUPS = TILES // 4
    FC = F // P
    UNITS = E * FC
    STEPS = 16
    assert KT == 8 and STEPS == 2 * (S // 512) * (KT // 2)
    V1 = 2 * K + 1

    ctx_dram = nc.dram_tensor("ctx_scratch", [TILES, P, HK], F32, kind="Internal").ap()
    x_tiles = x.rearrange("b (t p) d -> p (b t) d", p=P)
    out_tiles = out.rearrange("b (t p) d -> p (b t) d", p=P)

    stack = ExitStack()
    with stack:
        def sb(name, shape, dt, where=stack):
            return where.enter_context(nc.sbuf_tensor(name, shape, dt))

        def sem(name):
            return stack.enter_context(nc.semaphore(name))

        psum = stack.enter_context(nc.psum_tensor("psum", [P, 8, 512], F32))
        ident = sb("ident", [P, P], F32)
        xb = sb("xb", [P, TILES, D], F32)
        xnb = sb("xnb", [P, TILES, D], F32)
        xT_hi = sb("xT_hi", [P, TILES * P], F16)
        xT_lo = sb("xT_lo", [P, TILES * P], F16)
        w_hi = sb("w_hi", [P, 3, HK], F16)
        w_lo = sb("w_lo", [P, 3, HK], F16)
        bias_cols = sb("bias_cols", [P, 2 * PAIRS_PER_BATCH + UNITS], F32)
        gamma_b = sb("gamma_b", [P, D], F32)
        br_b = sb("br_b", [P, E], F32)
        wr_sb = sb("wr_sb", [P, E], F32)
        b2_sb = sb("b2_sb", [E, D], F32)
        neg_half = sb("neg_half", [P, TILES], F32)
        BK0, B10 = PAIRS_PER_BATCH, 2 * PAIRS_PER_BATCH

        early = ExitStack()
        stage = sb("stage", [P, 3, HK], F32, early)
        bias_rows = sb("bias_rows", [2 * PAIRS_PER_BATCH + UNITS, P], F32, early)
        bo_b = sb("bo_b", [P, D], F32, early)
        beta_b = sb("beta_b", [P, D], F32, early)
        bv_b = sb("bv_b", [P, HK], F32, early)
        st1 = sb("st1", [P, TILES, 6], F32, early)
        sm1 = sb("sm1", [P, 6, TILES], F32, early)
        chunk32 = sb("chunk32", [P, 2, 512], F32, early)
        q_nat = sb("q_nat", [P, 2, S], F16, early)
        k_nat = sb("k_nat", [P, 2, S], F16, early)
        v32 = sb("v32", [P, 2, 4, P], F32, early)
        q_stack = sb("q_stack", [P, 2, 2, S], F16, early)
        q_max = sb("q_max", [P, 2, 2, S], F16, early)
        k_stack = sb("k_stack", [P, 2, 2, S], F16, early)
        k_one = sb("k_one", [P, 2, 2, S], F16, early)
        v_ext = sb("v_ext", [P, 2, KT, 2, V1 + 1], F16, early)
        probs = sb("probs", [P, 4, 2, 512], F32, early)
        probs_lo = sb("probs_lo", [P, 4, 2, 512], F16, early)
        mcol = sb("mcol", [P, 2, KT], F32, early)
        mrow = sb("mrow", [KT, 2, P], F16, early)
        rden = sb("rden", [P, 2, 4], F32, early)
        ctx_sb = sb("ctx_sb", [P, 2, KT, P], F32, early)
        early.close()

        wo_hi = sb("wo_hi", [P, HK // P, D], F16)
        wo_lo = sb("wo_lo", [P, HK // P, D], F16)
        w1_hi = sb("w1_hi", [P, E, F], F16)
        w1_lo = sb("w1_lo", [P, E, F], F16)
        w2_hi = sb("w2_hi", [P, UNITS, D], F16)
        w2_lo = sb("w2_lo", [P, UNITS, D], F16)
        wstage = sb("wstage", [P, 2, 2048], F32)
        cx = sb("cx", [P, 4, HK], F32)
        cT_hi = sb("cT_hi", [P, 2, 512], F16)
        cT_lo = sb("cT_lo", [P, 2, 512], F16)
        y = sb("y", [P, 4, D], F32)
        z = sb("z", [P, 4, D], F32)
        zg = sb("zg", [P, 4, D], F32)
        st2 = sb("st2", [P, 4, 6], F32)
        sm2 = sb("sm2", [P, 6, 4], F32)
        x2 = sb("x2", [P, 4, D], F32)
        x2T = sb("x2T", [P, 4, P], F32)
        acc = sb("acc", [P, TILES, D], F32)
        lg = sb("lg", [P, 4, E], F32)
        lg2 = sb("lg2", [P, 4, E], F32)
        pe_ = sb("pe_", [P, 4, E], F32)
        pr = sb("pr", [P, 4, E], F32)
        top = sb("top", [P, 4, 8], F32)
        rest = sb("rest", [P, 4, E], F32)
        wsel = sb("wsel", [P, 4, E], F32)
        rt = sb("rt", [P, 4, E], F32)
        rs = sb("rs", [P, 4, 4], F32)
        rT = sb("rT", [E, 4, P], F32)
        h32 = sb("h32", [P, 4, 512], F32)
        h_lo = sb("h_lo", [P, 4, 512], F16)

        def high_half(ap):
            return ap.bitcast(BF16).rearrange("p (n two) -> p n two", two=2)[:, :, 1]

        def wait(eng, s, value):
            if not isinstance(value, int) or value > 0:
                eng.wait_ge(s, value)

        s_mark = sem("waits_passed")

        def waits_apart(eng, *waits):
            for s, v in waits:
                if not isinstance(v, int) or v > 0:
                    eng.wait_ge(s, v)
                    eng.sem_inc(s_mark, 1)

        def live(pair):
            return not isinstance(pair, int) or 0 <= pair < PAIRS

        class Chain:

            def __init__(self, eng, name):
                self.eng, self.sem, self.n = eng, sem(name), 0

            def __call__(self, ins):
                self.n += 1
                ins.then_inc(self.sem, 1)
                self.eng.wait_ge(self.sem, self.n)

        s_x = [sem(f"x_loaded{b}") for b in range(B)]
        s_w = sem("qkv_weights_loaded")
        s_rows = sem("bias_rows_loaded")
        s_small = sem("small_loaded")
        s_ident0, s_ident = sem("ident_cleared"), sem("ident_ready")
        s_half = sem("neg_half_ready")
        s_const0, s_const = sem("stack_rows_cleared"), sem("stack_rows_ready")
        s_var, s_rstd = sem("ln1_variance"), sem("ln1_rstd")
        s_xn = sem("ln1_tiles")
        s_bT, s_bc = sem("bias_transposed"), sem("bias_cols_ready")
        s_xT = sem("xT_in_psum")
        s_xTh, s_xTl = sem("xT_hi_ready"), sem("xT_lo_ready")
        s_wh, s_wl = sem("w_hi_ready"), sem("w_lo_ready")
        s_xpost = sem("x_plus_beta")
        s_bop = sem("bo_added")

        with nc.Block() as blk:
            @blk.sync
            def _(sp):
                for b in range(B):
                    sp.dma_start(xb[:, b * KT:(b + 1) * KT, :], x_tiles[:, b * KT:(b + 1) * KT, :]).then_inc(s_x[b], 16)
                for n, w in enumerate((Wq, Wk, Wv)):
                    sp.dma_start(stage[:, n, :], w.rearrange("d h k -> d (h k)")).then_inc(s_w, 16)

            @blk.scalar
            def _(act):
                nq = PAIRS_PER_BATCH
                act.dma_start(bias_rows[0:nq, :], bq.rearrange("(c h) k -> c (h k)", h=2)).then_inc(s_rows, 16)
                act.dma_start(bias_rows[nq:2 * nq, :], bk.rearrange("(c h) k -> c (h k)", h=2)).then_inc(s_rows, 16)
                act.dma_start(bias_rows[2 * nq:, :], b1.rearrange("e (c p) -> (e c) p", p=P)).then_inc(s_rows, 16)
                act.dma_start(bo_b[:], bo.unsqueeze(0).to_broadcast([P, D])).then_inc(s_small, 16)
                act.dma_start(beta_b[:], beta.unsqueeze(0).to_broadcast([P, D])).then_inc(s_small, 16)
                act.dma_start(gamma_b[:], gamma.unsqueeze(0).to_broadcast([P, D])).then_inc(s_small, 16)
                act.dma_start(br_b[:], br.unsqueeze(0).to_broadcast([P, E])).then_inc(s_small, 16)
                act.dma_start(bv_b[:], bv.rearrange("h k -> (h k)").unsqueeze(0).to_broadcast([P, HK])).then_inc(s_small, 16)
                act.dma_start(wr_sb[:], Wr).then_inc(s_small, 16)
                act.dma_start(b2_sb[:], b2).then_inc(s_small, 16)
                act.wait_ge(s_bT, 1)
                nc.scalar.activation(bias_cols[:, 0:BK0], psum[:, 7, 0:BK0], ACT.Copy, scale=SCALE)
                nc.scalar.activation(bias_cols[:, BK0:], psum[:, 7, BK0:B10 + UNITS], ACT.Copy).then_inc(s_bc, 1)
                act.wait_ge(s_w, 48)
                for n in range(3):
                    nc.scalar.activation(w_hi[:, n, :], stage[:, n, :], ACT.Copy,
                                         scale=SCALE if n == 0 else 1.0).then_inc(s_wh, 1)
                for g in range(GROUPS):
                    act.wait_ge(s_xT, g + 1)
                    nc.scalar.activation(xT_hi[:, g * 512:(g + 1) * 512], psum[:, g, :], ACT.Copy).then_inc(s_xTh, 1)

            @blk.gpsimd
            def _(pool):
                nc.gpsimd.memset(ident[:], 0.0).then_inc(s_ident0, 1)
                nc.gpsimd.memset(neg_half[:], -0.5).then_inc(s_half, 1)
                pool.wait_ge(s_ident0, 1)
                nc.gpsimd.affine_select(out=ident[:], in_=ident[:], compare_op=ALU.not_equal, fill=1.0, base=0,
                                        pattern=[[-1, P]], channel_multiplier=1).then_inc(s_ident, 1)
                pool.wait_ge(s_half, 1)
                for b in range(B):
                    pool.wait_ge(s_var, b + 1)
                    t = slice(b * KT, (b + 1) * KT)
                    nc.gpsimd.tensor_tensor(sm1[:, 5, t], sm1[:, 4, t], neg_half[:, t], ALU.pow).then_inc(s_rstd, 1)

            @blk.tensor
            def _(pe):
                pe.wait_ge(s_ident, 1)
                pe.wait_ge(s_rows, 48)
                nb = 2 * PAIRS_PER_BATCH + UNITS
                pe.transpose(psum[:, 7, 0:nb], bias_rows[:, :], ident[0:nb, 0:nb]).then_inc(s_bT, 1)
                for g in range(GROUPS):
                    pe.wait_ge(s_xn, 4 * (g + 1))
                    if g == 7:
                        pe.wait_ge(s_bc, 1)
                    for t in range(4):
                        ins = pe.transpose(psum[:, g, t * P:(t + 1) * P], xnb[:, 4 * g + t, :], ident[:])
                    ins.then_inc(s_xT, 1)

            @blk.vector
            def _(dve):
                link = Chain(dve, "setup_chain")
                nc.vector.memset(k_one[K:P, :, :, :], 0.0).then_inc(s_const0, 1)
                nc.vector.memset(q_max[K:P, :, :, :], 0.0)
                nc.vector.memset(v_ext[:, :, :, :, K:K + 1], 1.0)
                dve.wait_ge(s_const0, 1)
                nc.vector.memset(k_one[K:K + 1, :, :, :], 1.0).then_inc(s_const, 1)
                for b in range(B):
                    dve.wait_ge(s_x[b], 16)
                    for t in range(b * KT, (b + 1) * KT):
                        ins = nc.vector.bn_stats(st1[:, t, :], xb[:, t, :])
                    link(ins)
                    tt = slice(b * KT, (b + 1) * KT)
                    me, mo = st1[:, tt, 1], st1[:, tt, 4]
                    nc.vector.tensor_tensor(sm1[:, 0, tt], me, mo, ALU.add)
                    nc.vector.tensor_tensor(sm1[:, 1, tt], me, mo, ALU.subtract)
                    link(nc.vector.tensor_tensor(sm1[:, 2, tt], st1[:, tt, 2], st1[:, tt, 5], ALU.add))
                    nc.vector.tensor_tensor(sm1[:, 3, tt], sm1[:, 1, tt], sm1[:, 1, tt], ALU.mult)
                    nc.vector.tensor_scalar(sm1[:, 0, tt], sm1[:, 0, tt], 0.5, None, ALU.mult)
                    link(nc.vector.tensor_scalar(sm1[:, 2, tt], sm1[:, 2, tt], 1.0 / D, LN_EPS, ALU.mult, ALU.add))
                    nc.vector.scalar_tensor_tensor(sm1[:, 4, tt], sm1[:, 3, tt], 0.25, sm1[:, 2, tt],
                                                   ALU.mult, ALU.add).then_inc(s_var, 1)
                for b in range(B):
                    dve.wait_ge(s_rstd, b + 1)
                    for t in range(b * KT, (b + 1) * KT):
                        nc.vector.tensor_scalar(xnb[:, t, :], xb[:, t, :], sm1[:, 0, t:t + 1], sm1[:, 5, t:t + 1],
                                                ALU.subtract, ALU.mult).then_inc(s_xn, 1)
                for n in range(3):
                    dve.wait_ge(s_wh, n + 1)
                    nc.vector.scalar_tensor_tensor(w_lo[:, n, :], stage[:, n, :], SCALE if n == 0 else 1.0,
                                                   w_hi[:, n, :], ALU.mult, ALU.subtract).then_inc(s_wl, 1)
                for g in range(GROUPS):
                    dve.wait_ge(s_xTh, g + 1)
                    c = slice(g * 512, (g + 1) * 512)
                    nc.vector.tensor_tensor(xT_lo[:, c], psum[:, g, :], xT_hi[:, c], ALU.subtract).then_inc(s_xTl, 1)
                dve.wait_ge(s_small, 7 * 16)
                dve.wait_ge(s_xn, TILES)
                nc.vector.tensor_tensor(xb[:], xb[:], beta_b[:].unsqueeze(1).to_broadcast([P, TILES, D]),
                                        ALU.add).then_inc(s_xpost, 1)
                dve.wait_ge(s_xT, GROUPS)
                nc.vector.tensor_tensor(xnb[:], xnb[:], bo_b[:].unsqueeze(1).to_broadcast([P, TILES, D]),
                                        ALU.add).then_inc(s_bop, 1)
                dve.wait_ge(s_const, 1)

        s_S = sem("scores_ready")
        s_mx = sem("max_scores_ready")
        s_mt = sem("max_transposed")
        s_pv = sem("context_step_done")
        s_pj = sem("projection_ready")
        s_exp = sem("exp_done")
        s_e32 = sem("chunk32_ready")
        s_hi = sem("qk_hi_ready")
        s_vh = sem("v_hi_ready")
        s_mr = sem("mrow_ready")
        s_red = sem("tile_max_done")
        s_qlo = sem("qk_lo_ready")
        s_v32 = sem("v32_ready")
        s_vlo = sem("v_lo_ready")
        s_rc = sem("reciprocal_done")
        s_ctx = sem("context_ready")
        s_lod = sem("probs_lo_by_vector")
        s_lop = sem("probs_lo_by_gpsimd")
        s_dq = sem("q_placed")
        s_dkh = sem("k_hi_placed")
        s_dkl = sem("k_lo_placed")
        s_dm = [sem(f"max_row_placed{h}") for h in range(2)]
        s_dc = [sem(f"context_stored{p}") for p in range(2)]

        PROJ = {0: 0, 1: 1, 2: 2, 3: 3, 9: 4, 10: 5}
        LAG = 3

        def max_tile(n, s):
            if s < 6:
                return n, 1, s + 2
            return (n + 1, 0, s - 6) if s < 14 else (n + 1, 1, s - 14)

        def lagged(n, s):
            return (n, s - LAG) if s >= LAG else (n - 1, s - LAG + STEPS)

        def pairs(eng, slots):
            slots(-1, 1)
            slots(0, 0)
            with eng.Fori(0, (PAIRS - 2) // 2) as j:
                for u in range(2):
                    slots(2 * j + 1 + u, (1 + u) % 2)
            slots(PAIRS - 1, 1)
            slots(PAIRS, 0)

        def where(m):
            return m // PAIRS_PER_BATCH, m % PAIRS_PER_BATCH

        with nc.Block() as blk:
            @blk.tensor
            def _(pe):
                def project(m, piece):
                    b, hp = where(m)
                    if piece < 4:
                        w, c = divmod(piece, 2)
                        wh, wl = (a[:, w, bass.ds(hp * P, P)] for a in (w_hi, w_lo))
                        xh, xl = (a[:, bass.ds(b * S + c * 512, 512)] for a in (xT_hi, xT_lo))
                        pe.matmul(psum[:, 7, :], wh, xh, start=True, stop=False)
                        pe.matmul(psum[:, 7, :], wh, xl, start=False, stop=False)
                        return pe.matmul(psum[:, 7, :], wl, xh, start=False, stop=True)
                    wh, wl = (a[:, 2, bass.ds(hp * P, P)] for a in (w_hi, w_lo))
                    for t in range(4):
                        xh, xl = (a[:, bass.ds(b * S + ((piece - 4) * 4 + t) * P, P)] for a in (xT_hi, xT_lo))
                        o = psum[:, 7, t * P:(t + 1) * P]
                        pe.matmul(o, xh, wh, start=True, stop=False)
                        pe.matmul(o, xh, wl, start=False, stop=False)
                        ins = pe.matmul(o, xl, wh, start=False, stop=True)
                    return ins

                def slots(n, par):
                    for s in range(STEPS):
                        g = STEPS * n + s
                        if live(n):
                            h, half, kp = s // 8, s // 4 % 2, s % 4
                            if s == 0:
                                pe.wait_ge(s_dkl, 32 * (n + 1))
                            if s % 8 == 0:
                                pe.wait_ge(s_dm[h], 16 * (n + 1))
                            wait(pe, s_exp, g - 1)
                            q = slice(half * 512, (half + 1) * 512)
                            for i in range(2):
                                k = slice((2 * kp + i) * P, (2 * kp + i + 1) * P)
                                o = psum[:, 2 * (s % 2) + i, :]
                                pe.matmul(o, k_stack[:, par, h, k], q_stack[:, par, h, q], start=True, stop=False)
                                ins = pe.matmul(o, k_one[:, par, h, k], q_max[:, par, h, q], start=False, stop=True)
                            ins.then_inc(s_S, 1)
                        m, h, t = max_tile(n, s)
                        if live(m):
                            mp = par if s < 6 else 1 - par
                            if s == 6:
                                pe.wait_ge(s_dq, 96 * (n + 2))
                                pe.wait_ge(s_dkh, 64 * (n + 2))
                            wait(pe, s_red, 10 + STEPS * n + s)
                            for i in range(2):
                                ins = pe.matmul(psum[:, 4 + i, :], q_stack[:, mp, h, t * P:(t + 1) * P],
                                                k_stack[:, mp, h, i * 512:(i + 1) * 512], start=True, stop=True)
                            ins.then_inc(s_mx, 1)
                        if s in PROJ and live(n + 1):
                            piece = PROJ[s]
                            if piece == 0:
                                wait(pe, s_mr, 2 * n + 1)
                            elif piece < 4:
                                pe.wait_ge(s_hi, 4 * (n + 1) + piece)
                            elif piece == 4:
                                pe.wait_ge(s_hi, 4 * (n + 2))
                                wait(pe, s_mr, 2 * n + 2)
                            else:
                                pe.wait_ge(s_v32, 2 * (n + 1) + 1)
                            project(n + 1, piece).then_inc(s_pj, 1)
                        if (s == 6 and live(n)) or (s == 14 and live(n + 1)):
                            h = 1 if s == 6 else 0
                            pe.wait_ge(s_red, (16 if s == 6 else 24) + STEPS * n)
                            if s == 14:
                                pe.wait_ge(s_v32, 2 * (n + 2))
                            elif live(n + 1):
                                pe.wait_ge(s_hi, 4 * (n + 2))
                            else:
                                pe.wait_ge(s_mr, 2 * n + 1)
                            pe.transpose(psum[0:KT, 7, 0:P], mcol[:, h, :], ident[:]).then_inc(s_mt, 1)
                        m, t = lagged(n, s)
                        if live(m):
                            gl = STEPS * m + t
                            vp = par if s >= LAG else 1 - par
                            h, kp = t // 8, t % 4
                            if t == 0:
                                pe.wait_ge(s_vh, 2 * (m + 1))
                                pe.wait_ge(s_vlo, 2 * (m + 1))
                            if kp == 0:
                                wait(pe, s_ctx, 4 * m + t // 4)
                            pe.wait_ge(s_exp, gl + 1)
                            if kp == 3:
                                pe.wait_ge(s_lod, 4 * m + t // 4 + 1)
                            else:
                                pe.wait_ge(s_lop, 12 * m + 3 * (t // 4) + kp + 1)
                            for i in range(2):
                                v = v_ext[:, vp, 2 * kp + i, h, :]
                                for qt in range(4):
                                    c = slice(qt * P, (qt + 1) * P)
                                    ph = high_half(probs[:, t % 4, i, :])[:, c]
                                    o = psum[:, 6, qt * (K + 1):(qt + 1) * (K + 1)]
                                    first = kp == 0 and i == 0 and qt == 0
                                    last = kp == 3 and i == 1
                                    pe.matmul(o, ph, v[:, 0:K + 1], start=first, stop=False, skip_group_check=True)
                                    pe.matmul(o[:, 0:K], ph, v[:, K + 1:V1], start=False, stop=False,
                                              skip_group_check=True)
                                    ins = pe.matmul(o, probs_lo[:, t % 4, i, c], v[:, 0:K + 1], start=False,
                                                    stop=last, skip_group_check=True)
                            ins.then_inc(s_pv, 1)

                pairs(pe, slots)

            @blk.scalar
            def _(act):
                def slots(n, par):
                    for s in range(STEPS):
                        g = STEPS * n + s
                        if live(n):
                            act.wait_ge(s_S, g + 1)
                            wait(act, s_pv, g - 3)
                            nc.scalar.activation(probs[:, s % 4, :, :], psum[:, 2 * (s % 2):2 * (s % 2) + 2, :],
                                                 ACT.Exp).then_inc(s_exp, 1)
                        if s < 4 and live(n + 1):
                            done = 4 * (n + 1) + s
                            w, c = divmod(s, 2)
                            bias = bias_cols[:, bass.ds(w * BK0 + where(n + 1)[1], 1)]
                            waits_apart(act, (s_pj, 6 * (n + 1) + s + 1), (s_qlo, done - 1))
                            nc.scalar.activation(chunk32[:, s % 2, :], psum[:, 7, :], ACT.Identity,
                                                 bias=bias).then_inc(s_e32, 1)
                            if s == 0:
                                waits_apart(act, (s_dq, 96 * (n + 1)))
                            if s == 2:
                                waits_apart(act, (s_dkh, 64 * (n + 1)))
                            nat = (q_nat, k_nat)[w]
                            nc.scalar.activation(nat[:, 0, c * 512:(c + 1) * 512], psum[:, 7, :], ACT.Identity,
                                                 bias=bias).then_inc(s_hi, 1)
                        if s in (10, 11) and live(n + 1):
                            c = s - 10
                            act.wait_ge(s_v32, 2 * (n + 1) + c + 1)
                            wait(act, s_pv, STEPS * n)
                            nc.scalar.activation(
                                v_ext[:, 1 - par, 4 * c:4 * c + 4, :, 0:K],
                                v32[:, c, :, :].rearrange("p t (h k) -> p t h k", h=2), ACT.Copy).then_inc(s_vh, 1)
                        if (s == 6 and live(n)) or (s == 14 and live(n + 1)):
                            h = 1 if s == 6 else 0
                            idx = 2 * n + 1 if s == 6 else 2 * n + 2
                            act.wait_ge(s_mt, idx + 1)
                            wait(act, s_dm[h], 16 * (n if s == 6 else n + 1))
                            nc.scalar.activation(mrow[:, h, :], psum[0:KT, 7, 0:P], ACT.Copy, bias=HEADROOM,
                                                 scale=-1.0).then_inc(s_mr, 1)

                pairs(act, slots)

            @blk.gpsimd
            def _(pool):
                def slots(n, par):
                    if not live(n):
                        return
                    for s in range(STEPS):
                        if s % 4 == 3:
                            continue
                        pool.wait_ge(s_exp, STEPS * n + s + 1)
                        p = probs[:, s % 4, :, :].rearrange("p a b -> p (a b)")
                        nc.gpsimd.tensor_tensor(probs_lo[:, s % 4, :, :].rearrange("p a b -> p (a b)"), p,
                                                high_half(p), ALU.subtract).then_inc(s_lop, 1)

                pairs(pool, slots)

            @blk.vector
            def _(dve):
                def slots(n, par):
                    for s in range(STEPS):
                        g = STEPS * n + s
                        if s % 4 == 3:
                            m, idx = (n, s // 4 - 1) if s > 3 else (n - 1, 3)
                            cp = par if s > 3 else 1 - par
                            if live(m):
                                done = 4 * m + idx
                                h, half = divmod(idx, 2)
                                dve.wait_ge(s_pv, 4 * (done + 1))
                                if idx == 0:
                                    wait(dve, s_dc[cp], 16 * (m // 2 + 1))
                                ps = psum[:, 6, 0:4 * (K + 1)].rearrange("p (t k) -> p t k", t=4)
                                nc.vector.reciprocal(rden[:, idx % 2, :], ps[:, :, K]).then_inc(s_rc, 1)
                                dve.wait_ge(s_rc, done + 1)
                                nc.vector.tensor_tensor(
                                    ctx_sb[:, cp, 4 * half:4 * half + 4, h * K:(h + 1) * K], ps[:, :, 0:K],
                                    rden[:, idx % 2, :].unsqueeze(2).to_broadcast([P, 4, K]),
                                    ALU.mult).then_inc(s_ctx, 1)
                        m, h, t = max_tile(n, s)
                        if live(m):
                            dve.wait_ge(s_mx, 11 + STEPS * n + s)
                            if s in (6, 14):
                                wait(dve, s_mt, 2 * n + (1 if s == 6 else 2))
                            nc.vector.reduce_max(mcol[:, h, t:t + 1], psum[:, 4:6, :], AX.XY).then_inc(s_red, 1)
                        if 1 <= s <= 4 and live(n + 1):
                            c = s - 1
                            dve.wait_ge(s_hi, 4 * (n + 1) + c + 1)
                            dve.wait_ge(s_e32, 4 * (n + 1) + c + 1)
                            if c == 0:
                                wait(dve, s_dq, 96 * (n + 1))
                            if c == 2:
                                wait(dve, s_dkl, 32 * (n + 1))
                            nat = (q_nat, k_nat)[c // 2]
                            o = slice((c % 2) * 512, (c % 2 + 1) * 512)
                            nc.vector.tensor_tensor(nat[:, 1, o], chunk32[:, c % 2, :], nat[:, 0, o],
                                                    ALU.subtract).then_inc(s_qlo, 1)
                        if s in (9, 10) and live(n + 1):
                            c = s - 9
                            dve.wait_ge(s_pj, 6 * (n + 1) + 4 + c + 1)
                            wait(dve, s_vlo, 2 * (n + 1))
                            wait(dve, s_vh, 2 * (n + 1))
                            b = bv_b[:, bass.ds(where(n + 1)[1] * P, P)].unsqueeze(1).to_broadcast([P, 4, P])
                            nc.vector.tensor_tensor(v32[:, c, :, :], psum[:, 7, :].rearrange("p (t k) -> p t k", t=4),
                                                    b, ALU.add).then_inc(s_v32, 1)
                        if s in (13, 14) and live(n + 1):
                            c = s - 13
                            dve.wait_ge(s_vh, 2 * (n + 1) + c + 1)
                            v = v32[:, c, :, :].rearrange("p t (h k) -> p t h k", h=2)
                            ve = v_ext[:, 1 - par, 4 * c:4 * c + 4, :, :]
                            nc.vector.tensor_tensor(ve[:, :, :, K + 1:V1], v, ve[:, :, :, 0:K],
                                                    ALU.subtract).then_inc(s_vlo, 1)
                        if s % 4 == 0 and (live(n - 1) if s == 0 else live(n)):
                            dve.wait_ge(s_exp, g)
                            p = probs[:, 3, :, :].rearrange("p a b -> p (a b)")
                            nc.vector.tensor_tensor(probs_lo[:, 3, :, :].rearrange("p a b -> p (a b)"), p,
                                                    high_half(p), ALU.subtract).then_inc(s_lod, 1)

                pairs(dve, slots)

            @blk.sync
            def _(sp):
                def slots(n, par):
                    nx = 1 - par
                    if live(n + 1):
                        waits_apart(sp, (s_hi, 4 * (n + 1) + 2), (s_S, STEPS * n))
                        for h in range(2):
                            r = slice(h * K, (h + 1) * K)
                            sp.dma_start(q_stack[0:K, nx, h, :], q_nat[r, 0, :]).then_inc(s_dq, 16)
                            sp.dma_start(q_max[0:K, nx, h, :], q_nat[r, 0, :]).then_inc(s_dq, 16)
                        sp.wait_ge(s_qlo, 4 * (n + 1) + 2)
                        for h in range(2):
                            sp.dma_start(q_stack[K:P, nx, h, :], q_nat[h * K:(h + 1) * K, 1, :]).then_inc(s_dq, 16)
                        sp.wait_ge(s_hi, 4 * (n + 1) + 4)
                        for h in range(2):
                            r = slice(h * K, (h + 1) * K)
                            sp.dma_start(k_stack[0:K, nx, h, :], k_nat[r, 0, :]).then_inc(s_dkh, 16)
                            sp.dma_start(k_stack[K:P, nx, h, :], k_nat[r, 0, :]).then_inc(s_dkh, 16)
                        sp.wait_ge(s_qlo, 4 * (n + 1) + 4)
                        for h in range(2):
                            sp.dma_start(k_one[0:K, nx, h, :], k_nat[h * K:(h + 1) * K, 1, :]).then_inc(s_dkl, 16)
                    if live(n - 1):
                        b, hp = where(n - 1)
                        waits_apart(sp, (s_ctx, 4 * n))
                        sp.dma_start(ctx_dram[bass.ds(b * KT, KT), :, bass.ds(hp * P, P)].rearrange("t p k -> p t k"),
                                     ctx_sb[:, nx, :, :]).then_inc(s_dc[nx], 16)
                    if live(n):
                        sp.wait_ge(s_mr, 2 * n + 2)
                        sp.dma_start(q_max[K:K + 1, par, 1, :], mrow[:, 1, :]).then_inc(s_dm[1], 16)
                    if live(n + 1):
                        sp.wait_ge(s_mr, 2 * n + 3)
                        sp.dma_start(q_max[K:K + 1, nx, 0, :], mrow[:, 0, :]).then_inc(s_dm[0], 16)

                for p in range(2):
                    sp.sem_inc(s_dc[p], 16)
                pairs(sp, slots)
                for p in range(2):
                    sp.wait_ge(s_dc[p], 16 * (PAIRS // 2 + 1))

        W_LOADS = [(W1.rearrange("e d f -> d e f")[:, 0:4, :], w1_hi[:, 0:4, :], w1_lo[:, 0:4, :]),
                   (W1.rearrange("e d f -> d e f")[:, 4:8, :], w1_hi[:, 4:8, :], w1_lo[:, 4:8, :]),
                   (W2.rearrange("e (c p) d -> p (e c) d", p=P)[:, 0:16, :], w2_hi[:, 0:16, :], w2_lo[:, 0:16, :]),
                   (W2.rearrange("e (c p) d -> p (e c) d", p=P)[:, 16:32, :], w2_hi[:, 16:32, :], w2_lo[:, 16:32, :])]
        WO = (Wo.rearrange("h k d -> (h k) d").rearrange("(c p) d -> p c d", p=P), wo_hi[:], wo_lo[:])
        LOADS = [WO] + W_LOADS
        s_wld = [sem(f"late_weights_loaded{i}") for i in range(2)]
        s_lwh, s_lwl = sem("late_w_hi"), sem("late_w_lo")
        s_cx = sem("ctx_loaded")
        s_ct = sem("ctx_transposed")
        s_cth = sem("ctx_T_hi")
        s_ctl = sem("ctx_T_lo")
        s_cm = sem("ctx_chunk_multiplied")
        s_ao = sem("attn_out_read")
        s_v2, s_r2 = sem("ln_variance"), sem("ln_rstd")
        s_z = sem("ln2_done")
        s_zg = sem("gamma_done")
        s_x1 = sem("x1_ready")
        s_x2 = sem("x2_ready")
        s_x2t = sem("x2_transposed")
        s_x2f, s_x2h, s_x2l = sem("x2T_f32"), sem("x2T_hi"), sem("x2T_lo")
        s_lg = sem("logits_ready")
        s_lgr = sem("logits_shifted")
        s_le = sem("logits_exp")
        s_rt = sem("routing_ready")
        s_rtt = sem("routing_transposed")
        s_rts = sem("routing_T_ready")
        s_b2 = sem("b2_term_ready")
        s_acc = sem("b2_term_added")
        s_h = sem("hidden_ready")
        s_h32 = sem("relu_done")
        s_hlv = sem("hidden_lo_by_vector")
        s_hlp = sem("hidden_lo_by_gpsimd")
        s_w2 = sem("unit_multiplied")
        s_cb = sem("expert_added")
        s_out = sem("out_stored")
        NC = HK // P
        HLAG = 3
        BY_VECTOR = 4
        T_SLOT = {1 + 2 * c: c for c in range(NC)}
        M_SLOT = {3 + 2 * c: c for c in range(NC)}
        X2T_SLOT, LOGIT_SLOT, RT_SLOT, B2_SLOT = 28, 30, 6, 8

        def groups(eng, slots):
            slots(-1)
            slots(0)
            with eng.Fori(1, GROUPS - 1) as g:
                slots(g)
            slots(GROUPS - 1)
            slots(GROUPS)

        def ok(g):
            return not isinstance(g, int) or 0 <= g < GROUPS

        def unit_at(g, s):
            return (g, s - HLAG) if s >= HLAG else (g - 1, s - HLAG + UNITS)

        with nc.Block() as blk:
            @blk.sync
            def _(sp):
                for i, (src, hi, _) in enumerate(LOADS):
                    n = hi.shape[1] * hi.shape[2]
                    if i >= 2:
                        sp.wait_ge(s_lwl, i - 1)
                    sp.dma_start(wstage[:, i % 2, 0:n].rearrange("p (a b) -> p a b", a=hi.shape[1]),
                                 src).then_inc(s_wld[i % 2], 16)
                    if i == 1:
                        sp.dma_start(cx[:], ctx_dram[0:4].rearrange("t p k -> p t k")).then_inc(s_cx, 16)

                def slots(g):
                    if ok(g) and ok(g + 1):
                        waits_apart(sp, (s_ct, NC * (g + 1)))
                    if ok(g + 1) and not (isinstance(g, int) and g < 0):
                        sp.dma_start(cx[:], ctx_dram[bass.ds(4 * (g + 1), 4)].rearrange("t p k -> p t k"))\
                            .then_inc(s_cx, 16)
                    if ok(g - 1):
                        waits_apart(sp, (s_cb, E * g))
                        sp.dma_start(out_tiles[:, bass.ds(4 * (g - 1), 4), :],
                                     acc[:, bass.ds(4 * (g - 1), 4), :]).then_inc(s_out, 16)

                groups(sp, slots)
                sp.wait_ge(s_out, 16 * GROUPS)

            @blk.tensor
            def _(pe):
                def slots(g):
                    for s in range(UNITS):
                        if ok(g):
                            u = UNITS * g + s
                            e, c = divmod(s, FC)
                            if s == 0:
                                pe.wait_ge(s_x2h, g + 1)
                                pe.wait_ge(s_x2l, g + 1)
                                if isinstance(g, int) and g == 0:
                                    pe.wait_ge(s_lwl, len(LOADS))
                            wait(pe, s_h32, u - 1 if s < 2 else u - 2)
                            xh, xl = (a[:, bass.ds(g * 512, 512)] for a in (xT_hi, xT_lo))
                            wh, wl = (a[:, e, c * P:(c + 1) * P] for a in (w1_hi, w1_lo))
                            o = psum[:, s % 3, :]
                            pe.matmul(o, wh, xh, start=True, stop=False)
                            pe.matmul(o, wh, xl, start=False, stop=False)
                            pe.matmul(o, wl, xh, start=False, stop=True).then_inc(s_h, 1)
                        if ok(g + 1) and s in T_SLOT:
                            c = T_SLOT[s]
                            if c == 0:
                                pe.wait_ge(s_cx, 16 * (g + 2))
                            wait(pe, s_ctl, NC * (g + 1) + c)
                            for t in range(4):
                                ins = pe.transpose(psum[:, 5, t * P:(t + 1) * P], cx[:, t, c * P:(c + 1) * P],
                                                   ident[:])
                            ins.then_inc(s_ct, 1)
                        if ok(g + 1) and s in M_SLOT:
                            c = M_SLOT[s]
                            pe.wait_ge(s_cth, NC * (g + 1) + c + 1)
                            pe.wait_ge(s_ctl, NC * (g + 1) + c + 1)
                            if c == 0:
                                wait(pe, s_ao, g + 1)
                                if isinstance(g, int) and g == -1:
                                    pe.wait_ge(s_lwl, 1)
                            for t in range(4):
                                o = psum[:, 6, t * P:(t + 1) * P]
                                ch, cl = (a[:, c % 2, t * P:(t + 1) * P] for a in (cT_hi, cT_lo))
                                pe.matmul(o, ch, wo_hi[:, c, :], start=(c == 0 and t == 0), stop=False,
                                          skip_group_check=True)
                                pe.matmul(o, ch, wo_lo[:, c, :], start=False, stop=False, skip_group_check=True)
                                ins = pe.matmul(o, cl, wo_hi[:, c, :], start=False, stop=(c == NC - 1),
                                                skip_group_check=True)
                            ins.then_inc(s_cm, 1)
                        if ok(g + 1) and s == X2T_SLOT:
                            pe.wait_ge(s_x2, g + 2)
                            wait(pe, s_acc, g + 1)
                            for t in range(4):
                                ins = pe.transpose(psum[:, 7, t * P:(t + 1) * P], x2[:, t, :], ident[:])
                            ins.then_inc(s_x2t, 1)
                        if ok(g + 1) and s == LOGIT_SLOT:
                            pe.wait_ge(s_x2f, g + 2)
                            pe.wait_ge(s_x2l, g + 2)
                            for t in range(4):
                                ins = pe.matmul(psum[:, 7, t * E:(t + 1) * E], x2T[:, t, :], wr_sb[:],
                                                start=True, stop=True)
                            ins.then_inc(s_lg, 1)
                        if ok(g) and s == RT_SLOT:
                            pe.wait_ge(s_rt, g + 1)
                            for t in range(4):
                                ins = pe.transpose(psum[0:E, 7, t * P:(t + 1) * P], rt[:, t, :], ident[:])
                            ins.then_inc(s_rtt, 1)
                        if ok(g) and s == B2_SLOT:
                            pe.wait_ge(s_rts, g + 1)
                            for t in range(4):
                                ins = pe.matmul(psum[:, 7, t * P:(t + 1) * P], rT[:, t, :], b2_sb[:],
                                                start=True, stop=True)
                            ins.then_inc(s_b2, 1)
                        m, t = unit_at(g, s)
                        if ok(m):
                            u = UNITS * m + t
                            e, c = divmod(t, FC)
                            if c == 0:
                                wait(pe, s_cb, E * m + e - 1)
                            pe.wait_ge(s_h32, u + 1)
                            if t % BY_VECTOR == BY_VECTOR - 1:
                                pe.wait_ge(s_hlv, m * (UNITS // BY_VECTOR) + t // BY_VECTOR + 1)
                            else:
                                pe.wait_ge(s_hlp, m * (UNITS - UNITS // BY_VECTOR) + t - t // BY_VECTOR + 1)
                            hh = high_half(h32[:, t % 4, :])
                            for tt in range(4):
                                o = psum[:, 3 + e % 2, tt * P:(tt + 1) * P]
                                r = slice(tt * P, (tt + 1) * P)
                                pe.matmul(o, hh[:, r], w2_hi[:, t, :], start=(c == 0 and tt == 0), stop=False,
                                          skip_group_check=True)
                                pe.matmul(o, hh[:, r], w2_lo[:, t, :], start=False, stop=False,
                                          skip_group_check=True)
                                ins = pe.matmul(o, h_lo[:, t % 4, r], w2_hi[:, t, :], start=False,
                                                stop=(c == FC - 1), skip_group_check=True)
                            ins.then_inc(s_w2, 1)

                groups(pe, slots)

            @blk.scalar
            def _(act):
                def split(i):
                    _, hi, _ = LOADS[i]
                    act.wait_ge(s_wld[i % 2], 16 * (i // 2 + 1))
                    n = hi.shape[1] * hi.shape[2]
                    nc.scalar.activation(hi, wstage[:, i % 2, 0:n].rearrange("p (a b) -> p a b", a=hi.shape[1]),
                                         ACT.Copy).then_inc(s_lwh, 1)

                split(0)

                def slots(g):
                    for s in range(UNITS):
                        if ok(g):
                            u = UNITS * g + s
                            act.wait_ge(s_h, u + 1)
                            wait(act, s_w2, u - 3)
                            nc.scalar.activation(h32[:, s % 4, :], psum[:, s % 3, :], ACT.Relu,
                                                 bias=bias_cols[:, B10 + s:B10 + s + 1]).then_inc(s_h32, 1)
                        if ok(g + 1) and s in T_SLOT:
                            c = T_SLOT[s]
                            act.wait_ge(s_ct, NC * (g + 1) + c + 1)
                            wait(act, s_cm, NC * (g + 1) + c - 1)
                            nc.scalar.activation(cT_hi[:, c % 2, :], psum[:, 5, :], ACT.Copy).then_inc(s_cth, 1)
                            if isinstance(g, int) and g == -1 and c % 2 == 1:
                                split(c // 2 + 1)
                        if ok(g + 1) and s == X2T_SLOT:
                            waits_apart(act, (s_x2t, g + 2), (s_lg, g + 1))
                            nc.scalar.activation(x2T[:].rearrange("p t k -> p (t k)"), psum[:, 7, :],
                                                 ACT.Copy).then_inc(s_x2f, 1)
                            nc.scalar.activation(xT_hi[:, bass.ds((g + 1) * 512, 512)], psum[:, 7, :],
                                                 ACT.Copy).then_inc(s_x2h, 1)
                        if ok(g) and s == 0:
                            act.wait_ge(s_lgr, g + 1)
                            nc.scalar.activation(pe_[:], lg2[:], ACT.Exp).then_inc(s_le, 1)
                        if ok(g) and s == RT_SLOT:
                            act.wait_ge(s_rtt, g + 1)
                            wait(act, s_b2, g)
                            nc.scalar.activation(rT[:].rearrange("e t k -> e (t k)"), psum[0:E, 7, :],
                                                 ACT.Copy).then_inc(s_rts, 1)

                groups(act, slots)

            @blk.gpsimd
            def _(pool):
                def slots(g):
                    for s in range(UNITS):
                        if ok(g) and s % BY_VECTOR != BY_VECTOR - 1:
                            pool.wait_ge(s_h32, UNITS * g + s + 1)
                            nc.gpsimd.tensor_tensor(h_lo[:, s % 4, :], h32[:, s % 4, :], high_half(h32[:, s % 4, :]),
                                                    ALU.subtract).then_inc(s_hlp, 1)
                        if ok(g + 1) and s == 18:
                            pool.wait_ge(s_v2, 2 * (g + 1) + 1)
                            nc.gpsimd.tensor_tensor(sm2[:, 5, :], sm2[:, 4, :], neg_half[:, 0:4],
                                                    ALU.pow).then_inc(s_r2, 1)
                        if ok(g + 1) and s == 20:
                            pool.wait_ge(s_z, g + 2)
                            nc.gpsimd.tensor_tensor(zg[:], z[:], gamma_b[:].unsqueeze(1).to_broadcast([P, 4, D]),
                                                    ALU.mult).then_inc(s_zg, 1)
                            pool.wait_ge(s_zg, g + 2)
                            nc.gpsimd.tensor_tensor(acc[:, bass.ds(4 * (g + 1), 4), :], zg[:],
                                                    xb[:, bass.ds(4 * (g + 1), 4), :], ALU.add).then_inc(s_x1, 1)
                        if ok(g + 1) and s == 24:
                            pool.wait_ge(s_v2, 2 * (g + 1) + 2)
                            nc.gpsimd.tensor_tensor(sm2[:, 5, :], sm2[:, 4, :], neg_half[:, 0:4],
                                                    ALU.pow).then_inc(s_r2, 1)

                groups(pool, slots)

            @blk.vector
            def _(dve):
                s_ch = sem("vector_chain")

                def link(ins, g, i):
                    ins.then_inc(s_ch, 1)
                    if i in (10, 12):
                        waits_apart(dve, (s_ch, CHAIN * g + i + 1))
                    else:
                        dve.wait_ge(s_ch, CHAIN * g + i + 1)

                def split(i):
                    _, hi, lo = LOADS[i]
                    n = hi.shape[1] * hi.shape[2]
                    dve.wait_ge(s_lwh, i + 1)
                    nc.vector.tensor_tensor(lo, wstage[:, i % 2, 0:n].rearrange("p (a b) -> p a b", a=hi.shape[1]),
                                            hi, ALU.subtract).then_inc(s_lwl, 1)

                split(0)

                def stats(src, g, i0):
                    for t in range(4):
                        ins = nc.vector.bn_stats(st2[:, t, :], src[t])
                    link(ins, g, i0)
                    me, mo = st2[:, :, 1], st2[:, :, 4]
                    nc.vector.tensor_tensor(sm2[:, 0, :], me, mo, ALU.add)
                    nc.vector.tensor_tensor(sm2[:, 1, :], me, mo, ALU.subtract)
                    link(nc.vector.tensor_tensor(sm2[:, 2, :], st2[:, :, 2], st2[:, :, 5], ALU.add), g, i0 + 1)
                    nc.vector.tensor_tensor(sm2[:, 3, :], sm2[:, 1, :], sm2[:, 1, :], ALU.mult)
                    nc.vector.tensor_scalar(sm2[:, 0, :], sm2[:, 0, :], 0.5, None, ALU.mult)
                    eps = ATTN_EPS if i0 == 0 else LN_EPS
                    link(nc.vector.tensor_scalar(sm2[:, 2, :], sm2[:, 2, :], 1.0 / D, eps, ALU.mult, ALU.add),
                         g, i0 + 2)
                    nc.vector.scalar_tensor_tensor(sm2[:, 4, :], sm2[:, 3, :], 0.25, sm2[:, 2, :], ALU.mult,
                                                   ALU.add).then_inc(s_v2, 1)

                CHAIN = 17

                def add_expert(m, e):
                    dve.wait_ge(s_w2, UNITS * m + FC * (e + 1))
                    wait(dve, s_cb, E * m + e)
                    dve.wait_ge(s_rt, m + 1)
                    if e == 1:
                        dve.wait_ge(s_acc, m + 1)
                    for t in range(4):
                        a = acc[:, bass.ds(4 * m + t, 1), :].rearrange("p a d -> p (a d)")
                        ins = nc.vector.scalar_tensor_tensor(a, psum[:, 3 + e % 2, t * P:(t + 1) * P],
                                                             rt[:, t, e:e + 1], a, ALU.mult, ALU.add)
                    ins.then_inc(s_cb, 1)

                def slots(g):
                    for s in range(UNITS):
                        if s == 3 and ok(g - 1):
                            add_expert(g - 1, E - 1)
                        if ok(g + 1) and s in T_SLOT:
                            c = T_SLOT[s]
                            dve.wait_ge(s_cth, NC * (g + 1) + c + 1)
                            nc.vector.tensor_tensor(cT_lo[:, c % 2, :], psum[:, 5, :], cT_hi[:, c % 2, :],
                                                    ALU.subtract).then_inc(s_ctl, 1)
                            if isinstance(g, int) and g == -1 and c % 2 == 1:
                                split(c // 2 + 1)
                        if ok(g) and s % BY_VECTOR == 0 and s > 0:
                            low(g, s - 1)
                        if ok(g - 1) and s == 0:
                            low(g - 1, UNITS - 1)
                        if ok(g) and s > 4 and s % FC == 3:
                            add_expert(g, s // FC - 1)
                        if ok(g + 1) and s == 18:
                            dve.wait_ge(s_cm, NC * (g + 2))
                            nc.vector.tensor_tensor(y[:], psum[:, 6, :].rearrange("p (t d) -> p t d", t=4),
                                                    xnb[:, bass.ds(4 * (g + 1), 4), :], ALU.add).then_inc(s_ao, 1)
                            dve.wait_ge(s_ao, g + 2)
                            stats([y[:, t, :] for t in range(4)], g + 1, 0)
                        if ok(g + 1) and s == 20:
                            dve.wait_ge(s_r2, 2 * (g + 1) + 1)
                            for t in range(4):
                                ins = nc.vector.tensor_scalar(z[:, t, :], y[:, t, :], sm2[:, 0, t:t + 1],
                                                              sm2[:, 5, t:t + 1], ALU.subtract, ALU.mult)
                            ins.then_inc(s_z, 1)
                        if ok(g + 1) and s == 24:
                            dve.wait_ge(s_x1, g + 2)
                            dve.wait_ge(s_z, g + 2)
                            stats([acc[:, bass.ds(4 * (g + 1) + t, 1), :].rearrange("p a d -> p (a d)")
                                   for t in range(4)], g + 1, 3)
                        if ok(g + 1) and s == 26:
                            dve.wait_ge(s_r2, 2 * (g + 1) + 2)
                            for t in range(4):
                                a = acc[:, bass.ds(4 * (g + 1) + t, 1), :].rearrange("p a d -> p (a d)")
                                ins = nc.vector.tensor_scalar(x2[:, t, :], a, sm2[:, 0, t:t + 1],
                                                              sm2[:, 5, t:t + 1], ALU.subtract, ALU.mult)
                            ins.then_inc(s_x2, 1)
                        if ok(g + 1) and s == X2T_SLOT:
                            dve.wait_ge(s_x2h, g + 2)
                            c = bass.ds((g + 1) * 512, 512)
                            nc.vector.tensor_tensor(xT_lo[:, c], psum[:, 7, :], xT_hi[:, c],
                                                    ALU.subtract).then_inc(s_x2l, 1)
                        if ok(g + 1) and s == 31:
                            dve.wait_ge(s_lg, g + 2)
                            link(nc.vector.tensor_tensor(lg[:], psum[:, 7, 0:4 * E].rearrange("p (t e) -> p t e", t=4),
                                                         br_b[:].unsqueeze(1).to_broadcast([P, 4, E]), ALU.add),
                                 g + 1, 6)
                            link(nc.vector.reduce_max(rs[:, 0, :], lg[:], AX.X), g + 1, 7)
                            nc.vector.tensor_tensor(lg2[:], lg[:], rs[:, 0, :].unsqueeze(2).to_broadcast([P, 4, E]),
                                                    ALU.subtract).then_inc(s_lgr, 1)
                        if ok(g) and s == 3:
                            routing(g)
                        if ok(g) and s == B2_SLOT + 1:
                            dve.wait_ge(s_b2, g + 1)
                            dve.wait_ge(s_cb, E * g + 1)
                            a = acc[:, bass.ds(4 * g, 4), :]
                            nc.vector.tensor_tensor(a, psum[:, 7, :].rearrange("p (t d) -> p t d", t=4), a,
                                                    ALU.add).then_inc(s_acc, 1)

                def low(m, t):
                    dve.wait_ge(s_h32, UNITS * m + t + 1)
                    nc.vector.tensor_tensor(h_lo[:, t % 4, :], h32[:, t % 4, :], high_half(h32[:, t % 4, :]),
                                            ALU.subtract).then_inc(s_hlv, 1)

                def routing(g):
                    dve.wait_ge(s_le, g + 1)
                    link(nc.vector.reduce_sum(rs[:, 1, :], pe_[:], AX.X), g, 8)
                    link(nc.vector.reciprocal(rs[:, 2, :], rs[:, 1, :]), g, 9)
                    link(nc.vector.tensor_tensor(pr[:], pe_[:], rs[:, 2, :].unsqueeze(2).to_broadcast([P, 4, E]),
                                                 ALU.mult), g, 10)
                    for t in range(4):
                        ins = nc.vector.max(top[:, t, :], pr[:, t, :])
                    link(ins, g, 11)
                    link(nc.vector.memset(top[:, :, 2:8], -1.0), g, 12)
                    for t in range(4):
                        ins = nc.vector.match_replace(out=rest[:, t, :], in_to_replace=top[:, t, :],
                                                      in_values=pr[:, t, :], imm_value=0.0)
                    link(ins, g, 13)
                    link(nc.vector.tensor_tensor(wsel[:], pr[:], rest[:], ALU.subtract), g, 14)
                    link(nc.vector.reduce_sum(rs[:, 3, :], wsel[:], AX.X), g, 15)
                    link(nc.vector.reciprocal(rs[:, 3, :], rs[:, 3, :]), g, 16)
                    nc.vector.tensor_tensor(rt[:], wsel[:], rs[:, 3, :].unsqueeze(2).to_broadcast([P, 4, E]),
                                            ALU.mult).then_inc(s_rt, 1)

                groups(dve, slots)


_INS = ["L0_attn_x", "L0_attn_Wq", "L0_attn_bq", "L0_attn_Wk", "L0_attn_bk", "L0_attn_Wv", "L0_attn_bv", "L0_attn_Wo",
        "L0_attn_bo", "L0_attn_gamma", "L0_attn_beta", "L0_ffn_W1", "L0_ffn_b1", "L0_ffn_W2", "L0_ffn_b2",
        "L0_ffn_Wr", "L0_ffn_br"]


def kernel(**inputs):
    import numpy as np
    import concourse.bacc as bacc
    from concourse.bass_utils import run_bass_kernel_spmd

    nc = bacc.Bacc("TRN2", target_bir_lowering=False, num_devices=1)
    arrays, args = {}, []
    for name in _INS:
        a = np.ascontiguousarray(inputs[name])
        arrays[f"in_{name}"] = a
        args.append(nc.dram_tensor(f"in_{name}", a.shape, mybir.dt.from_np(a.dtype), kind="ExternalInput").ap())
    out = nc.dram_tensor("out_0", inputs["L0_attn_x"].shape, F32, kind="ExternalOutput").ap()
    block_kernel(nc, *args, out)
    r = run_bass_kernel_spmd(nc, [arrays], core_ids=[0])
    return r.results[0]["out_0"]
```

```python
from contextlib import ExitStack

import concourse.bass as bass
from concourse import mybir

ALU = mybir.AluOpType
ACT = mybir.ActivationFunctionType
AX = mybir.AxisListType
F32 = mybir.dt.float32
F16 = mybir.dt.float16
BF16 = mybir.dt.bfloat16

P = 128


def block_kernel(nc, x, Wq, bq, Wk, bk, Wv, bv, Wo, bo, gamma, beta, W1, b1, W2, b2, Wr, br, out):
    B, S, D = x.shape
    H, K = Wq.shape[1:]
    E, _, F = W1.shape
    assert D == P and 2 * K == P and S % 512 == 0
    ATTN_EPS, LN_EPS = 1e-3, 1e-5
    SCALE = K ** -0.5
    HEADROOM = 8.0
    TILES = B * S // P
    PAIRS_PER_BATCH = H // 2
    PAIRS = B * PAIRS_PER_BATCH
    KT = S // P
    HK = H * K
    GROUPS = TILES // 4
    FC = F // P
    UNITS = E * FC
    STEPS = 16
    assert KT == 8 and STEPS == 2 * (S // 512) * (KT // 2)
    RINGS = 4 * 1024 * 6
    PAD = (RINGS - 4 * 512 * 6 - 4 * P * 4 - 8 * 128 - 64) // 4
    V1 = 2 * K + 1

    ctx_dram = nc.dram_tensor("ctx_scratch", [TILES, P, HK], F32, kind="Internal").ap()
    x_tiles = x.rearrange("b (t p) d -> p (b t) d", p=P)
    out_tiles = out.rearrange("b (t p) d -> p (b t) d", p=P)

    stack = ExitStack()
    with stack:
        def sb(name, shape, dt, where=stack):
            return where.enter_context(nc.sbuf_tensor(name, shape, dt))

        def sem(name):
            return stack.enter_context(nc.semaphore(name))

        psum = stack.enter_context(nc.psum_tensor("psum", [P, 8, 512], F32))
        ident = sb("ident", [P, P], F32)
        xb = sb("xb", [P, TILES, D], F32)
        xnb = sb("xnb", [P, TILES, D], F32)
        xT_hi = sb("xT_hi", [P, TILES * P], F16)
        xT_lo = sb("xT_lo", [P, TILES * P], F16)
        bias_cols = sb("bias_cols", [P, 2 * PAIRS_PER_BATCH + UNITS], F32)
        gamma_b = sb("gamma_b", [P, D], F32)
        beta_b = sb("beta_b", [P, D], F32)
        bo_b = sb("bo_b", [P, D], F32)
        br_b = sb("br_b", [P, E], F32)
        wr_sb = sb("wr_sb", [P, E], F32)
        b2_sb = sb("b2_sb", [E, D], F32)
        neg_half = sb("neg_half", [P, TILES], F32)
        BK0, B10 = PAIRS_PER_BATCH, 2 * PAIRS_PER_BATCH
        wo_hi = sb("wo_hi", [P, HK // P, D], F16)
        wo_lo = sb("wo_lo", [P, HK // P, D], F16)
        w1_hi = sb("w1_hi", [P, E, F], F16)
        w1_lo = sb("w1_lo", [P, E, F], F16)
        w2_hi = sb("w2_hi", [P, UNITS, D], F16)
        w2_lo = sb("w2_lo", [P, UNITS, D], F16)
        stage = sb("stage", [P, 3, HK], F32)
        bias_rows = sb("bias_rows", [2 * PAIRS_PER_BATCH + UNITS, P], F32)
        st1 = sb("st1", [P, TILES, 6], F32)
        sm1 = sb("sm1", [P, 6, TILES], F32)
        q_stack = sb("q_stack", [P, 2, 2, S], F16)
        q_max = sb("q_max", [P, 2, 2, S], F16)
        k_stack = sb("k_stack", [P, 2, 2, S], F16)
        k_one = sb("k_one", [P, 2, 2, S], F16)
        v_ext = sb("v_ext", [P, 2, KT, 2, V1 + 1], F16)
        ctx_sb = sb("ctx_sb", [P, 2, KT, P], F32)
        mcol = sb("mcol", [P, 2, KT], F32)
        mrow = sb("mrow", [KT, 2, P], F16)
        rden = sb("rden", [P, 2, 4], F32)

        with ExitStack() as attention:
            probs = sb("probs", [P, 4, 2, 512], F32, attention)
            probs_lo = sb("probs_lo", [P, 4, 2, 512], F16, attention)
            w_hi = sb("w_hi", [P, 3, HK], F16, attention)
            w_lo = sb("w_lo", [P, 3, HK], F16, attention)
            chunk32 = sb("chunk32", [P, 2, 512], F32, attention)
            q_nat = sb("q_nat", [P, 2, S], F16, attention)
            k_nat = sb("k_nat", [P, 2, S], F16, attention)
            v32 = sb("v32", [P, 2, 4, P], F32, attention)
            bv_b = sb("bv_b", [P, HK], F32, attention)
        h32 = sb("h32", [P, 4, 512], F32)
        h_lo = sb("h_lo", [P, 4, 512], F16)
        rT = sb("rT", [E, 4, P], F32)
        lg = sb("lg", [P, 4, E], F32)
        lg2 = sb("lg2", [P, 4, E], F32)
        pe_ = sb("pe_", [P, 4, E], F32)
        pr = sb("pr", [P, 4, E], F32)
        top = sb("top", [P, 4, 8], F32)
        rest = sb("rest", [P, 4, E], F32)
        wsel = sb("wsel", [P, 4, E], F32)
        rt = sb("rt", [P, 4, E], F32)
        rs = sb("rs", [P, 4, 4], F32)
        pad = sb("pad", [P, PAD], F32)
        cx = sb("cx", [P, 4, HK], F32)
        cT_hi = sb("cT_hi", [P, 2, 512], F16)
        cT_lo = sb("cT_lo", [P, 2, 512], F16)
        y = sb("y", [P, 4, D], F32)
        z = sb("z", [P, 4, D], F32)
        x2 = sb("x2", [P, 4, D], F32)
        x2T = sb("x2T", [P, 4, P], F32)
        st2 = sb("st2", [P, 4, 6], F32)
        sm2 = sb("sm2", [P, 6, 4], F32)

        def high_half(ap):
            return ap.bitcast(BF16).rearrange("p (n two) -> p n two", two=2)[:, :, 1]

        def wait(eng, s, value):
            if not isinstance(value, int) or value > 0:
                eng.wait_ge(s, value)

        s_mark = sem("waits_passed")

        def waits_apart(eng, *waits):
            for s, v in waits:
                if not isinstance(v, int) or v > 0:
                    eng.wait_ge(s, v)
                    eng.sem_inc(s_mark, 1)

        def live(pair):
            return not isinstance(pair, int) or 0 <= pair < PAIRS

        class Chain:

            def __init__(self, eng, name):
                self.eng, self.sem, self.n = eng, sem(name), 0

            def __call__(self, ins):
                self.n += 1
                ins.then_inc(self.sem, 1)
                self.eng.wait_ge(self.sem, self.n)

        s_x = [sem(f"x_loaded{b}") for b in range(B)]
        s_w = [sem(f"qkv_weights_loaded{n}") for n in range(3)]
        s_rows = sem("bias_rows_loaded")
        s_small = sem("small_loaded")
        s_ident0, s_ident = sem("ident_cleared"), sem("ident_ready")
        s_half = sem("neg_half_ready")
        s_const0, s_const = sem("stack_rows_cleared"), sem("stack_rows_ready")
        s_var, s_rstd = sem("ln1_variance"), sem("ln1_rstd")
        s_xn = sem("ln1_tiles")
        s_shift = sem("ln1_shift")
        s_bT, s_bc = sem("bias_transposed"), sem("bias_cols_ready")
        s_xT = sem("xT_in_psum")
        s_xTh, s_xTl = sem("xT_hi_ready"), sem("xT_lo_ready")
        s_wh, s_wl = sem("w_hi_ready"), sem("w_lo_ready")

        LATE = [(Wo.rearrange("h k d -> (h k) d").rearrange("(c p) d -> p c d", p=P), wo_hi[:], wo_lo[:])]
        for i in range(4):
            c = slice(2 * i, 2 * i + 2)
            LATE.append((W1.rearrange("e d f -> d e f")[:, c, :], w1_hi[:, c, :], w1_lo[:, c, :]))
        for i in range(4):
            c = slice(8 * i, 8 * i + 8)
            LATE.append((W2.rearrange("e (c p) d -> p (e c) d", p=P)[:, c, :], w2_hi[:, c, :], w2_lo[:, c, :]))
        s_late = [sem(f"late_weights_loaded{i}") for i in range(3)]
        s_lwh, s_lwl = sem("late_w_hi"), sem("late_w_lo")

        def late_stage(i):
            hi = LATE[i][1]
            return stage[:, i % 3, :].rearrange("p (a b) -> p a b", a=hi.shape[1])

        LATE_SLOTS = [6, 7, 8, 9, 12, STEPS + 2, STEPS + 6, STEPS + 10, STEPS + 14]
        XT_BANK = [0, 1, 2, 3, 6, 2, 3, 6]

        def setup_sync(sp):
            def load_x(b):
                sp.dma_start(xb[:, b * KT:(b + 1) * KT, :], x_tiles[:, b * KT:(b + 1) * KT, :]).then_inc(s_x[b], 16)

            load_x(0)
            for n, w in enumerate((Wq, Wk, Wv)):
                sp.dma_start(stage[:, n, :], w.rearrange("d h k -> d (h k)")).then_inc(s_w[n], 16)
            for b in range(1, B):
                load_x(b)

        def setup_scalar(act):
            nq = PAIRS_PER_BATCH
            act.dma_start(bias_rows[0:nq, :], bq.rearrange("(c h) k -> c (h k)", h=2)).then_inc(s_rows, 16)
            act.dma_start(bias_rows[nq:2 * nq, :], bk.rearrange("(c h) k -> c (h k)", h=2)).then_inc(s_rows, 16)
            act.dma_start(bias_rows[2 * nq:, :], b1.rearrange("e (c p) -> (e c) p", p=P)).then_inc(s_rows, 16)
            act.dma_start(bv_b[:], bv.rearrange("h k -> (h k)").unsqueeze(0).to_broadcast([P, HK])).then_inc(s_small, 16)
            for to, src in ((bo_b, bo), (beta_b, beta), (gamma_b, gamma), (br_b, br)):
                act.dma_start(to[:], src.unsqueeze(0).to_broadcast([P, src.shape[0]])).then_inc(s_small, 16)
            act.dma_start(wr_sb[:], Wr).then_inc(s_small, 16)
            act.dma_start(b2_sb[:], b2).then_inc(s_small, 16)
            act.wait_ge(s_bT, 1)
            nc.scalar.activation(bias_cols[:, 0:BK0], psum[:, 7, 0:BK0], ACT.Copy, scale=SCALE)
            nc.scalar.activation(bias_cols[:, BK0:], psum[:, 7, BK0:B10 + UNITS], ACT.Copy).then_inc(s_bc, 1)
            for n in range(3):
                act.wait_ge(s_w[n], 16)
                nc.scalar.activation(w_hi[:, n, :], stage[:, n, :], ACT.Copy,
                                     scale=SCALE if n == 0 else 1.0).then_inc(s_wh, 1)

            def x_high(g):
                act.wait_ge(s_xT, g + 1)
                nc.scalar.activation(xT_hi[:, g * 512:(g + 1) * 512], psum[:, XT_BANK[g], :],
                                     ACT.Copy).then_inc(s_xTh, 1)

            x_high(0)
            x_high(1)
            act.wait_ge(s_bc, 1)

            def early(s):
                if s == 5:
                    act.wait_ge(s_shift, 1)
                    for t in range((B - 1) * KT, B * KT):
                        nc.scalar.activation(xnb[:, t, :], xb[:, t, :], ACT.Identity, bias=sm1[:, 3, t:t + 1],
                                             scale=sm1[:, 5, t:t + 1]).then_inc(s_xn, 1)
                if 5 <= s < 11:
                    x_high(s - 3)
                if s in LATE_SLOTS:
                    i = LATE_SLOTS.index(s)
                    act.wait_ge(s_late[i % 3], 16 * (i // 3 + 1))
                    nc.scalar.activation(LATE[i][1], late_stage(i), ACT.Copy).then_inc(s_lwh, 1)

            return early

        def setup_gpsimd(pool):
            nc.gpsimd.memset(ident[:], 0.0).then_inc(s_ident0, 1)
            nc.gpsimd.memset(neg_half[:], -0.5).then_inc(s_half, 1)
            pool.wait_ge(s_ident0, 1)
            nc.gpsimd.affine_select(out=ident[:], in_=ident[:], compare_op=ALU.not_equal, fill=1.0, base=0,
                                    pattern=[[-1, P]], channel_multiplier=1).then_inc(s_ident, 1)
            pool.wait_ge(s_half, 1)

            def rstd(b):
                pool.wait_ge(s_var, b + 1)
                t = slice(b * KT, (b + 1) * KT)
                nc.gpsimd.tensor_tensor(sm1[:, 5, t], sm1[:, 4, t], neg_half[:, t], ALU.pow).then_inc(s_rstd, 1)

            def load(i):
                pool.dma_start(late_stage(i), LATE[i][0]).then_inc(s_late[i % 3], 16)

            rstd(0)
            for i in range(3):
                pool.wait_ge(s_wl, i + 1)
                load(i)
            for b in range(1, B):
                rstd(b)

            def late_low(i):
                pool.wait_ge(s_lwh, i + 1)
                hi, lo = LATE[i][1:]
                nc.gpsimd.tensor_tensor(lo, late_stage(i), hi, ALU.subtract).then_inc(s_lwl, 1)
                if i + 3 < len(LATE):
                    pool.wait_ge(s_lwl, i + 1)
                    load(i + 3)

            for i in range(5):
                late_low(i)
            pool.wait_ge(s_small, 7 * 16)

            def early(s):
                if s - 1 in LATE_SLOTS[5:]:
                    late_low(LATE_SLOTS.index(s - 1))

            return early

        def setup_tensor(pe):
            pe.wait_ge(s_ident, 1)
            pe.wait_ge(s_rows, 48)
            nb = 2 * PAIRS_PER_BATCH + UNITS
            pe.transpose(psum[:, 7, 0:nb], bias_rows[:, :], ident[0:nb, 0:nb]).then_inc(s_bT, 1)

            def x_turn(g):
                pe.wait_ge(s_xn, 4 * (g + 1))
                if g >= 5:
                    pe.wait_ge(s_xTl, g - 2)
                for t in range(4):
                    ins = pe.transpose(psum[:, XT_BANK[g], t * P:(t + 1) * P], xnb[:, 4 * g + t, :], ident[:])
                ins.then_inc(s_xT, 1)

            x_turn(0)
            x_turn(1)
            pe.wait_ge(s_wl, 3)
            pe.wait_ge(s_xTl, 2)
            pe.wait_ge(s_bc, 1)
            pe.wait_ge(s_small, 7 * 16)

            def early(s):
                if 5 <= s < 11:
                    x_turn(s - 3)

            return early

        def setup_vector(dve):
            link = Chain(dve, "setup_chain")
            nc.vector.memset(k_one[K:P, :, :, :], 0.0).then_inc(s_const0, 1)
            nc.vector.memset(q_max[K:P, :, :, :], 0.0)
            nc.vector.memset(v_ext[:, :, :, :, K:K + 1], 1.0)

            ONES = {12: 0, 13: 1, STEPS + 1: 2, STEPS + 6: 3}

            def statistics(b):
                dve.wait_ge(s_x[b], 16)
                for t in range(b * KT, (b + 1) * KT):
                    ins = nc.vector.bn_stats(st1[:, t, :], xb[:, t, :])
                link(ins)
                tt = slice(b * KT, (b + 1) * KT)
                me, mo = st1[:, tt, 1], st1[:, tt, 4]
                nc.vector.tensor_tensor(sm1[:, 0, tt], me, mo, ALU.add)
                nc.vector.tensor_tensor(sm1[:, 1, tt], me, mo, ALU.subtract)
                link(nc.vector.tensor_tensor(sm1[:, 2, tt], st1[:, tt, 2], st1[:, tt, 5], ALU.add))
                nc.vector.tensor_tensor(sm1[:, 3, tt], sm1[:, 1, tt], sm1[:, 1, tt], ALU.mult)
                nc.vector.tensor_scalar(sm1[:, 0, tt], sm1[:, 0, tt], 0.5, None, ALU.mult)
                link(nc.vector.tensor_scalar(sm1[:, 2, tt], sm1[:, 2, tt], 1.0 / D, LN_EPS, ALU.mult, ALU.add))
                nc.vector.scalar_tensor_tensor(sm1[:, 4, tt], sm1[:, 3, tt], 0.25, sm1[:, 2, tt],
                                               ALU.mult, ALU.add).then_inc(s_var, 1)

            def normalise(b):
                dve.wait_ge(s_rstd, b + 1)
                for t in range(b * KT, (b + 1) * KT):
                    nc.vector.tensor_scalar(xnb[:, t, :], xb[:, t, :], sm1[:, 0, t:t + 1], sm1[:, 5, t:t + 1],
                                            ALU.subtract, ALU.mult).then_inc(s_xn, 1)

            def shift(b):
                dve.wait_ge(s_rstd, b + 1)
                tt = slice(b * KT, (b + 1) * KT)
                nc.vector.scalar_tensor_tensor(sm1[:, 3, tt], sm1[:, 0, tt], -1.0, sm1[:, 5, tt], ALU.mult,
                                               ALU.mult).then_inc(s_shift, 1)

            def x_low(g):
                dve.wait_ge(s_xTh, g + 1)
                c = slice(g * 512, (g + 1) * 512)
                nc.vector.tensor_tensor(xT_lo[:, c], psum[:, XT_BANK[g], :], xT_hi[:, c],
                                        ALU.subtract).then_inc(s_xTl, 1)

            statistics(0)
            normalise(0)
            for n in range(3):
                dve.wait_ge(s_wh, n + 1)
                nc.vector.scalar_tensor_tensor(w_lo[:, n, :], stage[:, n, :], SCALE if n == 0 else 1.0,
                                               w_hi[:, n, :], ALU.mult, ALU.subtract).then_inc(s_wl, 1)
            x_low(0)
            x_low(1)
            dve.wait_ge(s_small, 7 * 16)
            dve.wait_ge(s_const0, 1)

            def early(s):
                if s in ONES:
                    nc.vector.memset(k_one[K:K + 1, ONES[s] // 2, ONES[s] % 2, :], 1.0).then_inc(s_const, 1)
                if s < 6:
                    (statistics, normalise if s < 5 else shift)[s % 2](s // 2 + 1)
                elif s < 12:
                    x_low(s - 4)

            return early

        s_S = sem("scores_ready")
        s_mx = sem("max_scores_ready")
        s_mt = sem("max_transposed")
        s_pv = sem("context_step_done")
        s_pj = sem("projection_ready")
        s_exp = sem("exp_done")
        s_e32 = sem("chunk32_ready")
        s_hi = sem("qk_hi_ready")
        s_vh = sem("v_hi_ready")
        s_mr = sem("mrow_ready")
        s_red = sem("tile_max_done")
        s_qlo = sem("qk_lo_ready")
        s_v32 = sem("v32_ready")
        s_vlo = sem("v_lo_ready")
        s_rc = sem("reciprocal_done")
        s_ctx = sem("context_ready")
        s_lod = sem("probs_lo_by_vector")
        s_lop = sem("probs_lo_by_gpsimd")
        s_dq = sem("q_placed")
        s_dkh = sem("k_hi_placed")
        s_dkl = sem("k_lo_placed")
        s_dm = [sem(f"max_row_placed{h}") for h in range(2)]
        s_dc = [sem(f"context_stored{p}") for p in range(2)]

        PROJ = {0: 0, 1: 1, 2: 2, 3: 3, 9: 4, 10: 5}
        LOWS = {1: 0, 2: 1, 3: 2, 5: 3}
        LAG = 3

        def max_tile(n, s):
            if s < 6:
                return n, 1, s + 2
            return (n + 1, 0, s - 6) if s < 14 else (n + 1, 1, s - 14)

        def max_banks(n, s):
            first = 0 if isinstance(n, int) and n == -1 and s % 2 else 4
            return slice(first, first + 2)

        def lagged(n, s):
            return (n, s - LAG) if s >= LAG else (n - 1, s - LAG + STEPS)

        def pairs(eng, slots):
            slots(-1, 1)
            slots(0, 0)
            with eng.Fori(0, (PAIRS - 2) // 2) as j:
                for u in range(2):
                    slots(2 * j + 1 + u, (1 + u) % 2)
            slots(PAIRS - 1, 1)
            slots(PAIRS, 0)

        PREPARE = {6 + i: range(3 * i, 3 * i + 3) for i in range(6)}
        PREPARE.update({12: (18, 19), 14: range(20, 24), 15: (24, 25), 16: (26, 27), 17: (28, 29), 18: (30, 31)})

        def between(n, s, early, prepare):
            if not isinstance(n, int):
                return
            if n <= 0:
                early(STEPS * (n + 1) + s)
            for p in PREPARE.get(STEPS * (n - PAIRS + 1) + s, ()):
                prepare(-1, p)

        def where(m):
            return m // PAIRS_PER_BATCH, m % PAIRS_PER_BATCH

        def attention_tensor(pe, early, prepare):
            def project(m, piece):
                b, hp = where(m)
                if piece < 4:
                    w, c = divmod(piece, 2)
                    wh, wl = (a[:, w, bass.ds(hp * P, P)] for a in (w_hi, w_lo))
                    xh, xl = (a[:, bass.ds(b * S + c * 512, 512)] for a in (xT_hi, xT_lo))
                    pe.matmul(psum[:, 7, :], wh, xh, start=True, stop=False)
                    pe.matmul(psum[:, 7, :], wh, xl, start=False, stop=False)
                    return pe.matmul(psum[:, 7, :], wl, xh, start=False, stop=True)
                wh, wl = (a[:, 2, bass.ds(hp * P, P)] for a in (w_hi, w_lo))
                for t in range(4):
                    xh, xl = (a[:, bass.ds(b * S + ((piece - 4) * 4 + t) * P, P)] for a in (xT_hi, xT_lo))
                    o = psum[:, 7, t * P:(t + 1) * P]
                    pe.matmul(o, xh, wh, start=True, stop=False)
                    pe.matmul(o, xh, wl, start=False, stop=False)
                    ins = pe.matmul(o, xl, wh, start=False, stop=True)
                return ins

            def slots(n, par):
                for s in range(STEPS):
                    g = STEPS * n + s
                    if live(n):
                        h, half, kp = s // 8, s // 4 % 2, s % 4
                        if isinstance(n, int) and n == 0 and s == 0:
                            pe.wait_ge(s_xTl, GROUPS)
                            pe.wait_ge(s_red, 10)
                            pe.wait_ge(s_const, 2)
                        if isinstance(n, int) and n == 0 and s == STEPS - 1:
                            pe.wait_ge(s_const, 4)
                        if s == 0:
                            pe.wait_ge(s_dkl, 32 * (n + 1))
                        if s % 8 == 0:
                            pe.wait_ge(s_dm[h], 16 * (n + 1))
                        wait(pe, s_exp, g - 1)
                        q = slice(half * 512, (half + 1) * 512)
                        for i in range(2):
                            k = slice((2 * kp + i) * P, (2 * kp + i + 1) * P)
                            o = psum[:, 2 * (s % 2) + i, :]
                            pe.matmul(o, k_stack[:, par, h, k], q_stack[:, par, h, q], start=True, stop=False)
                            ins = pe.matmul(o, k_one[:, par, h, k], q_max[:, par, h, q], start=False, stop=True)
                        ins.then_inc(s_S, 1)
                    m, h, t = max_tile(n, s)
                    if live(m):
                        mp = par if s < 6 else 1 - par
                        if s == 6:
                            pe.wait_ge(s_dq, 96 * (n + 2))
                            pe.wait_ge(s_dkh, 64 * (n + 2))
                        wait(pe, s_red, s - 7 if isinstance(n, int) and n == -1 else 10 + STEPS * n + s)
                        for i in range(2):
                            ins = pe.matmul(psum[:, max_banks(n, s), :][:, i, :], q_stack[:, mp, h, t * P:(t + 1) * P],
                                            k_stack[:, mp, h, i * 512:(i + 1) * 512], start=True, stop=True)
                        ins.then_inc(s_mx, 1)
                    if s in PROJ and live(n + 1):
                        piece = PROJ[s]
                        if piece == 0:
                            wait(pe, s_mr, 2 * n + 1)
                        elif piece < 4:
                            pe.wait_ge(s_e32, 4 * (n + 1) + piece)
                        elif piece == 4:
                            pe.wait_ge(s_e32, 4 * (n + 2))
                            wait(pe, s_mr, 2 * n + 2)
                        else:
                            pe.wait_ge(s_v32, 2 * (n + 1) + 1)
                        project(n + 1, piece).then_inc(s_pj, 1)
                    if (s == 6 and live(n)) or (s == 14 and live(n + 1)):
                        h = 1 if s == 6 else 0
                        pe.wait_ge(s_red, (16 if s == 6 else 24) + STEPS * n)
                        if s == 14:
                            pe.wait_ge(s_v32, 2 * (n + 2))
                        elif live(n + 1):
                            pe.wait_ge(s_e32, 4 * (n + 2))
                        else:
                            pe.wait_ge(s_mr, 2 * n + 1)
                        pe.transpose(psum[0:KT, 7, 0:P], mcol[:, h, :], ident[:]).then_inc(s_mt, 1)
                    m, t = lagged(n, s)
                    if live(m):
                        gl = STEPS * m + t
                        vp = par if s >= LAG else 1 - par
                        h, kp = t // 8, t % 4
                        if t == 0:
                            pe.wait_ge(s_vh, 2 * (m + 1))
                            pe.wait_ge(s_vlo, 2 * (m + 1))
                        if kp == 0:
                            wait(pe, s_ctx, 4 * m + t // 4)
                        pe.wait_ge(s_exp, gl + 1)
                        if kp == 3:
                            pe.wait_ge(s_lod, 4 * m + t // 4 + 1)
                        else:
                            pe.wait_ge(s_lop, 12 * m + 3 * (t // 4) + kp + 1)
                        for i in range(2):
                            v = v_ext[:, vp, 2 * kp + i, h, :]
                            for qt in range(4):
                                c = slice(qt * P, (qt + 1) * P)
                                ph = high_half(probs[:, t % 4, i, :])[:, c]
                                o = psum[:, 6, qt * (K + 1):(qt + 1) * (K + 1)]
                                first = kp == 0 and i == 0 and qt == 0
                                last = kp == 3 and i == 1
                                pe.matmul(o, ph, v[:, 0:K + 1], start=first, stop=False, skip_group_check=True)
                                pe.matmul(o[:, 0:K], ph, v[:, K + 1:V1], start=False, stop=False,
                                          skip_group_check=True)
                                ins = pe.matmul(o, probs_lo[:, t % 4, i, c], v[:, 0:K + 1], start=False,
                                                stop=last, skip_group_check=True)
                        ins.then_inc(s_pv, 1)

                    between(n, s, early, prepare)

            pairs(pe, slots)

        def attention_scalar(act, early, prepare):
            def slots(n, par):
                for s in range(STEPS):
                    g = STEPS * n + s
                    if live(n):
                        act.wait_ge(s_S, g + 1)
                        wait(act, s_pv, g - 3)
                        nc.scalar.activation(probs[:, s % 4, :, :], psum[:, 2 * (s % 2):2 * (s % 2) + 2, :],
                                             ACT.Exp).then_inc(s_exp, 1)
                    if s < 4 and live(n + 1):
                        done = 4 * (n + 1) + s
                        w, c = divmod(s, 2)
                        bias = bias_cols[:, bass.ds(w * BK0 + where(n + 1)[1], 1)]
                        waits_apart(act, (s_pj, 6 * (n + 1) + s + 1), (s_qlo, done - 1))
                        if s == 0:
                            waits_apart(act, (s_dq, 96 * (n + 1)))
                        if s == 2:
                            waits_apart(act, (s_dkh, 64 * (n + 1)))
                        nat = (q_nat, k_nat)[w]
                        nc.scalar.activation(nat[:, 0, c * 512:(c + 1) * 512], psum[:, 7, :], ACT.Identity,
                                             bias=bias).then_inc(s_hi, 1)
                        nc.scalar.activation(chunk32[:, s % 2, :], psum[:, 7, :], ACT.Identity,
                                             bias=bias).then_inc(s_e32, 1)
                    if s in (10, 11) and live(n + 1):
                        c = s - 10
                        act.wait_ge(s_v32, 2 * (n + 1) + c + 1)
                        wait(act, s_pv, STEPS * n)
                        nc.scalar.activation(
                            v_ext[:, 1 - par, 4 * c:4 * c + 4, :, 0:K],
                            v32[:, c, :, :].rearrange("p t (h k) -> p t h k", h=2), ACT.Copy).then_inc(s_vh, 1)
                    if (s == 6 and live(n)) or (s == 14 and live(n + 1)):
                        h = 1 if s == 6 else 0
                        idx = 2 * n + 1 if s == 6 else 2 * n + 2
                        act.wait_ge(s_mt, idx + 1)
                        wait(act, s_dm[h], 16 * (n if s == 6 else n + 1))
                        nc.scalar.activation(mrow[:, h, :], psum[0:KT, 7, 0:P], ACT.Copy, bias=HEADROOM,
                                             scale=-1.0).then_inc(s_mr, 1)

                    between(n, s, early, prepare)

            pairs(act, slots)

        def attention_gpsimd(pool, early, prepare):
            def slots(n, par):
                for s in range(STEPS):
                    if live(n) and s % 4 != 3:
                        pool.wait_ge(s_exp, STEPS * n + s + 1)
                        p = probs[:, s % 4, :, :].rearrange("p a b -> p (a b)")
                        nc.gpsimd.tensor_tensor(probs_lo[:, s % 4, :, :].rearrange("p a b -> p (a b)"), p,
                                                high_half(p), ALU.subtract).then_inc(s_lop, 1)
                    between(n, s, early, prepare)

            pairs(pool, slots)

        def attention_vector(dve, early, prepare):
            def slots(n, par):
                for s in range(STEPS):
                    g = STEPS * n + s
                    if s % 4 == 3:
                        m, idx = (n, s // 4 - 1) if s > 3 else (n - 1, 3)
                        cp = par if s > 3 else 1 - par
                        if live(m):
                            done = 4 * m + idx
                            h, half = divmod(idx, 2)
                            dve.wait_ge(s_pv, 4 * (done + 1))
                            if idx == 0:
                                wait(dve, s_dc[cp], 16 * (m // 2 + 1))
                            ps = psum[:, 6, 0:4 * (K + 1)].rearrange("p (t k) -> p t k", t=4)
                            nc.vector.reciprocal(rden[:, idx % 2, :], ps[:, :, K]).then_inc(s_rc, 1)
                            dve.wait_ge(s_rc, done + 1)
                            nc.vector.tensor_tensor(
                                ctx_sb[:, cp, 4 * half:4 * half + 4, h * K:(h + 1) * K], ps[:, :, 0:K],
                                rden[:, idx % 2, :].unsqueeze(2).to_broadcast([P, 4, K]),
                                ALU.mult).then_inc(s_ctx, 1)
                    m, h, t = max_tile(n, s)
                    if live(m):
                        dve.wait_ge(s_mx, 11 + STEPS * n + s)
                        if s in (6, 14):
                            wait(dve, s_mt, 2 * n + (1 if s == 6 else 2))
                        nc.vector.reduce_max(mcol[:, h, t:t + 1], psum[:, max_banks(n, s), :],
                                             AX.XY).then_inc(s_red, 1)
                    if s in LOWS and live(n + 1):
                        c = LOWS[s]
                        dve.wait_ge(s_hi, 4 * (n + 1) + c + 1)
                        dve.wait_ge(s_e32, 4 * (n + 1) + c + 1)
                        if c == 0:
                            wait(dve, s_dq, 96 * (n + 1))
                        if c == 2:
                            wait(dve, s_dkl, 32 * (n + 1))
                        nat = (q_nat, k_nat)[c // 2]
                        o = slice((c % 2) * 512, (c % 2 + 1) * 512)
                        nc.vector.tensor_tensor(nat[:, 1, o], chunk32[:, c % 2, :], nat[:, 0, o],
                                                ALU.subtract).then_inc(s_qlo, 1)
                    if s in (9, 10) and live(n + 1):
                        c = s - 9
                        dve.wait_ge(s_pj, 6 * (n + 1) + 4 + c + 1)
                        wait(dve, s_vlo, 2 * (n + 1))
                        wait(dve, s_vh, 2 * (n + 1))
                        b = bv_b[:, bass.ds(where(n + 1)[1] * P, P)].unsqueeze(1).to_broadcast([P, 4, P])
                        nc.vector.tensor_tensor(v32[:, c, :, :], psum[:, 7, :].rearrange("p (t k) -> p t k", t=4),
                                                b, ALU.add).then_inc(s_v32, 1)
                    if s in (13, 15) and live(n + 1):
                        c = (s - 13) // 2
                        dve.wait_ge(s_vh, 2 * (n + 1) + c + 1)
                        v = v32[:, c, :, :].rearrange("p t (h k) -> p t h k", h=2)
                        ve = v_ext[:, 1 - par, 4 * c:4 * c + 4, :, :]
                        nc.vector.tensor_tensor(ve[:, :, :, K + 1:V1], v, ve[:, :, :, 0:K],
                                                ALU.subtract).then_inc(s_vlo, 1)
                    if s % 4 == 0 and (live(n - 1) if s == 0 else live(n)):
                        dve.wait_ge(s_exp, g)
                        p = probs[:, 3, :, :].rearrange("p a b -> p (a b)")
                        nc.vector.tensor_tensor(probs_lo[:, 3, :, :].rearrange("p a b -> p (a b)"), p,
                                                high_half(p), ALU.subtract).then_inc(s_lod, 1)

                    between(n, s, early, prepare)

            pairs(dve, slots)

        def attention_sync(sp):
            def slots(n, par):
                nx = 1 - par
                if live(n + 1):
                    waits_apart(sp, (s_hi, 4 * (n + 1) + 2), (s_S, STEPS * n))
                    for h in range(2):
                        r = slice(h * K, (h + 1) * K)
                        sp.dma_start(q_stack[0:K, nx, h, :], q_nat[r, 0, :]).then_inc(s_dq, 16)
                        sp.dma_start(q_max[0:K, nx, h, :], q_nat[r, 0, :]).then_inc(s_dq, 16)
                    sp.wait_ge(s_qlo, 4 * (n + 1) + 2)
                    for h in range(2):
                        sp.dma_start(q_stack[K:P, nx, h, :], q_nat[h * K:(h + 1) * K, 1, :]).then_inc(s_dq, 16)
                    sp.wait_ge(s_hi, 4 * (n + 1) + 4)
                    for h in range(2):
                        r = slice(h * K, (h + 1) * K)
                        sp.dma_start(k_stack[0:K, nx, h, :], k_nat[r, 0, :]).then_inc(s_dkh, 16)
                        sp.dma_start(k_stack[K:P, nx, h, :], k_nat[r, 0, :]).then_inc(s_dkh, 16)
                if isinstance(n, int) and n == PAIRS - 1:
                    sp.wait_ge(s_pj, 6 * PAIRS)
                    for s_done, count in ((s_hi, 4), (s_qlo, 4), (s_vh, 2), (s_vlo, 2)):
                        sp.wait_ge(s_done, count * PAIRS)
                    for s_done, count in ((s_dq, 96), (s_dkh, 64), (s_dkl, 32)):
                        sp.wait_ge(s_done, count * PAIRS)
                    for p in range(2):
                        sp.wait_ge(s_dc[p], 16 * (PAIRS_PER_BATCH // 2 + 1))
                    sp.dma_start(cx[:], ctx_dram[0:4].rearrange("t p k -> p t k")).then_inc(s_cx, 16)
                if live(n - 1):
                    b, hp = where(n - 1)
                    waits_apart(sp, (s_ctx, 4 * n))
                    sp.dma_start(ctx_dram[bass.ds(b * KT, KT), :, bass.ds(hp * P, P)].rearrange("t p k -> p t k"),
                                 ctx_sb[:, nx, :, :]).then_inc(s_dc[nx], 16)
                if live(n):
                    sp.wait_ge(s_mr, 2 * n + 2)
                    sp.dma_start(q_max[K:K + 1, par, 1, :], mrow[:, 1, :]).then_inc(s_dm[1], 16)
                if live(n + 1):
                    sp.wait_ge(s_qlo, 4 * (n + 1) + 4)
                    for h in range(2):
                        sp.dma_start(k_one[0:K, nx, h, :], k_nat[h * K:(h + 1) * K, 1, :]).then_inc(s_dkl, 16)
                    sp.wait_ge(s_mr, 2 * n + 3)
                    sp.dma_start(q_max[K:K + 1, nx, 0, :], mrow[:, 0, :]).then_inc(s_dm[0], 16)
                if isinstance(n, int) and n == PAIRS - 1:
                    sp.wait_ge(s_ct, NC)
                    sp.dma_start(cx[:], ctx_dram[4:8].rearrange("t p k -> p t k")).then_inc(s_cx, 16)

            for p in range(2):
                sp.sem_inc(s_dc[p], 16)
            pairs(sp, slots)
            for p in range(2):
                sp.wait_ge(s_dc[p], 16 * (PAIRS // 2 + 1))

        s_cx = sem("ctx_loaded")
        s_ct = sem("ctx_transposed")
        s_cth = sem("ctx_T_hi")
        s_ctl = sem("ctx_T_lo")
        s_cm = sem("ctx_chunk_multiplied")
        s_ao = sem("attn_out_read")
        s_bo, s_beta = sem("bo_added"), sem("beta_added")
        s_v2, s_r2 = sem("ln_variance"), sem("ln_rstd")
        s_z = sem("gamma_term_done")
        s_x1 = sem("x1_ready")
        s_x2 = sem("x2_ready")
        s_x2t = sem("x2_transposed")
        s_x2f, s_x2h, s_x2l = sem("x2T_f32"), sem("x2T_hi"), sem("x2T_lo")
        s_lg = sem("logits_ready")
        s_lgr = sem("logits_shifted")
        s_le = sem("logits_exp")
        s_rt = sem("routing_ready")
        s_rtt = sem("routing_transposed")
        s_rts = sem("routing_T_ready")
        s_b2 = sem("b2_term_ready")
        s_acc = sem("b2_term_added")
        s_h = sem("hidden_ready")
        s_h32 = sem("relu_done")
        s_hlv = sem("hidden_lo_by_vector")
        s_hlp = sem("hidden_lo_by_gpsimd")
        s_w2 = sem("unit_multiplied")
        s_cb = sem("expert_added")
        s_out = sem("out_stored")
        NC = HK // P
        HLAG = 3
        BY_VECTOR = 4
        T_SLOT = {1 + 2 * c: c for c in range(NC)}
        M_SLOT = {3 + 2 * c: c for c in range(NC)}
        X2T_SLOT, LOGIT_SLOT, RT_SLOT, B2_SLOT = 28, 30, 6, 8

        def groups(eng, slot):
            def slots(g):
                for s in range(UNITS):
                    slot(g, s)

            slots(0)
            with eng.Fori(1, GROUPS - 1) as g:
                slots(g)
            slots(GROUPS - 1)
            slots(GROUPS)

        def ATTN_OUT(g):
            return 4 if isinstance(g, int) and g == 0 else 6

        def ok(g):
            return not isinstance(g, int) or 0 <= g < GROUPS

        def unit_at(g, s):
            return (g, s - HLAG) if s >= HLAG else (g - 1, s - HLAG + UNITS)

        def experts_sync(sp):
            def slots(g):
                if not (isinstance(g, int) and g == 0) and ok(g) and ok(g + 1):
                    waits_apart(sp, (s_ct, NC * (g + 1)))
                    sp.dma_start(cx[:], ctx_dram[bass.ds(4 * (g + 1), 4)].rearrange("t p k -> p t k"))\
                        .then_inc(s_cx, 16)
                if ok(g - 1):
                    waits_apart(sp, (s_cb, E * g))
                    sp.dma_start(out_tiles[:, bass.ds(4 * (g - 1), 4), :],
                                 xb[:, bass.ds(4 * (g - 1), 4), :]).then_inc(s_out, 16)

            slots(0)
            with sp.Fori(1, GROUPS - 1) as g:
                slots(g)
            slots(GROUPS - 1)
            slots(GROUPS)
            sp.wait_ge(s_out, 16 * GROUPS)

        def experts_tensor(pe):
            def slot(g, s):
                if ok(g):
                    u = UNITS * g + s
                    e, c = divmod(s, FC)
                    if s == 0:
                        pe.wait_ge(s_x2h, g + 1)
                        pe.wait_ge(s_x2l, g + 1)
                        if isinstance(g, int) and g == 0:
                            pe.wait_ge(s_exp, STEPS * PAIRS)
                    wait(pe, s_h32, u - 1 if s < 2 else u - 2)
                    xh, xl = (a[:, bass.ds(g * 512, 512)] for a in (xT_hi, xT_lo))
                    wh, wl = (a[:, e, c * P:(c + 1) * P] for a in (w1_hi, w1_lo))
                    o = psum[:, s % 3, :]
                    pe.matmul(o, wh, xh, start=True, stop=False)
                    pe.matmul(o, wh, xl, start=False, stop=False)
                    pe.matmul(o, wl, xh, start=False, stop=True).then_inc(s_h, 1)
                if ok(g + 1) and s in T_SLOT:
                    c = T_SLOT[s]
                    if c == 0:
                        pe.wait_ge(s_cx, 16 * (g + 2))
                        if isinstance(g, int) and g == -1:
                            pe.wait_ge(s_red, STEPS * PAIRS)
                    wait(pe, s_ctl, NC * (g + 1) + c)
                    for t in range(4):
                        ins = pe.transpose(psum[:, 5, t * P:(t + 1) * P], cx[:, t, c * P:(c + 1) * P],
                                           ident[:])
                    ins.then_inc(s_ct, 1)
                if ok(g + 1) and s in M_SLOT:
                    c = M_SLOT[s]
                    pe.wait_ge(s_cth, NC * (g + 1) + c + 1)
                    pe.wait_ge(s_ctl, NC * (g + 1) + c + 1)
                    if c == 0:
                        wait(pe, s_ao, g + 1)
                        if isinstance(g, int) and g == -1:
                            pe.wait_ge(s_lwl, len(LATE))
                        if isinstance(g, int) and g == 0:
                            pe.wait_ge(s_ctx, 4 * PAIRS)
                    for t in range(4):
                        o = psum[:, ATTN_OUT(g + 1), t * P:(t + 1) * P]
                        ch, cl = (a[:, c % 2, t * P:(t + 1) * P] for a in (cT_hi, cT_lo))
                        pe.matmul(o, ch, wo_hi[:, c, :], start=(c == 0 and t == 0), stop=False,
                                  skip_group_check=True)
                        pe.matmul(o, ch, wo_lo[:, c, :], start=False, stop=False, skip_group_check=True)
                        ins = pe.matmul(o, cl, wo_hi[:, c, :], start=False, stop=(c == NC - 1),
                                        skip_group_check=True)
                    ins.then_inc(s_cm, 1)
                if ok(g + 1) and s == X2T_SLOT:
                    pe.wait_ge(s_x2, g + 2)
                    wait(pe, s_acc, g + 1)
                    if isinstance(g, int) and g == -1:
                        pe.wait_ge(s_mr, 2 * PAIRS)
                    for t in range(4):
                        ins = pe.transpose(psum[:, 7, t * P:(t + 1) * P], x2[:, t, :], ident[:])
                    ins.then_inc(s_x2t, 1)
                if ok(g + 1) and s == LOGIT_SLOT:
                    pe.wait_ge(s_x2f, g + 2)
                    pe.wait_ge(s_x2l, g + 2)
                    for t in range(4):
                        ins = pe.matmul(psum[:, 7, t * E:(t + 1) * E], x2T[:, t, :], wr_sb[:],
                                        start=True, stop=True)
                    ins.then_inc(s_lg, 1)
                if ok(g) and s == RT_SLOT:
                    pe.wait_ge(s_rt, g + 1)
                    for t in range(4):
                        ins = pe.transpose(psum[0:E, 7, t * P:(t + 1) * P], rt[:, t, :], ident[:])
                    ins.then_inc(s_rtt, 1)
                if ok(g) and s == B2_SLOT:
                    pe.wait_ge(s_rts, g + 1)
                    for t in range(4):
                        ins = pe.matmul(psum[:, 7, t * P:(t + 1) * P], rT[:, t, :], b2_sb[:],
                                        start=True, stop=True)
                    ins.then_inc(s_b2, 1)
                m, t = unit_at(g, s)
                if ok(m):
                    u = UNITS * m + t
                    e, c = divmod(t, FC)
                    if c == 0:
                        wait(pe, s_cb, E * m + e - 1)
                    pe.wait_ge(s_h32, u + 1)
                    if t % BY_VECTOR == BY_VECTOR - 1:
                        pe.wait_ge(s_hlv, m * (UNITS // BY_VECTOR) + t // BY_VECTOR + 1)
                    else:
                        pe.wait_ge(s_hlp, m * (UNITS - UNITS // BY_VECTOR) + t - t // BY_VECTOR + 1)
                    hh = high_half(h32[:, t % 4, :])
                    for tt in range(4):
                        o = psum[:, 3 + e % 2, tt * P:(tt + 1) * P]
                        r = slice(tt * P, (tt + 1) * P)
                        pe.matmul(o, hh[:, r], w2_hi[:, t, :], start=(c == 0 and tt == 0), stop=False,
                                  skip_group_check=True)
                        pe.matmul(o, hh[:, r], w2_lo[:, t, :], start=False, stop=False,
                                  skip_group_check=True)
                        ins = pe.matmul(o, h_lo[:, t % 4, r], w2_hi[:, t, :], start=False,
                                        stop=(c == FC - 1), skip_group_check=True)
                    ins.then_inc(s_w2, 1)

            return slot

        def experts_scalar(act):
            def slot(g, s):
                if ok(g):
                    u = UNITS * g + s
                    act.wait_ge(s_h, u + 1)
                    if isinstance(g, int) and g == 0 and s == 0:
                        act.wait_ge(s_pv, STEPS * PAIRS)
                    wait(act, s_w2, u - 3)
                    nc.scalar.activation(h32[:, s % 4, :], psum[:, s % 3, :], ACT.Relu,
                                         bias=bias_cols[:, B10 + s:B10 + s + 1]).then_inc(s_h32, 1)
                if ok(g + 1) and s in T_SLOT:
                    c = T_SLOT[s]
                    act.wait_ge(s_ct, NC * (g + 1) + c + 1)
                    wait(act, s_cm, NC * (g + 1) + c - 1)
                    nc.scalar.activation(cT_hi[:, c % 2, :], psum[:, 5, :], ACT.Copy).then_inc(s_cth, 1)
                if ok(g + 1) and s == X2T_SLOT:
                    waits_apart(act, (s_x2t, g + 2), (s_lg, g + 1))
                    nc.scalar.activation(x2T[:].rearrange("p t k -> p (t k)"), psum[:, 7, :],
                                         ACT.Copy).then_inc(s_x2f, 1)
                    nc.scalar.activation(xT_hi[:, bass.ds((g + 1) * 512, 512)], psum[:, 7, :],
                                         ACT.Copy).then_inc(s_x2h, 1)
                if ok(g) and s == 0:
                    act.wait_ge(s_lgr, g + 1)
                    nc.scalar.activation(pe_[:], lg2[:], ACT.Exp).then_inc(s_le, 1)
                if ok(g) and s == RT_SLOT:
                    act.wait_ge(s_rtt, g + 1)
                    wait(act, s_b2, g)
                    nc.scalar.activation(rT[:].rearrange("e t k -> e (t k)"), psum[0:E, 7, :],
                                         ACT.Copy).then_inc(s_rts, 1)

            return slot

        def experts_gpsimd(pool):
            def slot(g, s):
                if ok(g) and s % BY_VECTOR != BY_VECTOR - 1:
                    pool.wait_ge(s_h32, UNITS * g + s + 1)
                    nc.gpsimd.tensor_tensor(h_lo[:, s % 4, :], h32[:, s % 4, :], high_half(h32[:, s % 4, :]),
                                            ALU.subtract).then_inc(s_hlp, 1)
                if ok(g + 1) and s == 4:
                    if isinstance(g, int) and g == -1:
                        pool.wait_ge(s_xT, GROUPS)
                        pool.wait_ge(s_xn, TILES)
                    a = xnb[:, bass.ds(4 * (g + 1), 4), :]
                    nc.gpsimd.tensor_tensor(a, a, bo_b[:].unsqueeze(1).to_broadcast([P, 4, D]),
                                            ALU.add).then_inc(s_bo, 1)
                if ok(g + 1) and s == 8:
                    a = xb[:, bass.ds(4 * (g + 1), 4), :]
                    nc.gpsimd.tensor_tensor(a, a, beta_b[:].unsqueeze(1).to_broadcast([P, 4, D]),
                                            ALU.add).then_inc(s_beta, 1)
                if ok(g + 1) and s == 18:
                    pool.wait_ge(s_v2, 2 * (g + 1) + 1)
                    nc.gpsimd.tensor_tensor(sm2[:, 5, :], sm2[:, 4, :], neg_half[:, 0:4],
                                            ALU.pow).then_inc(s_r2, 1)
                if ok(g + 1) and s == 24:
                    pool.wait_ge(s_v2, 2 * (g + 1) + 2)
                    nc.gpsimd.tensor_tensor(sm2[:, 5, :], sm2[:, 4, :], neg_half[:, 0:4],
                                            ALU.pow).then_inc(s_r2, 1)

            return slot

        def experts_vector(dve):
            s_ch = sem("vector_chain")
            CHAIN = 17

            def link(ins, g, i):
                ins.then_inc(s_ch, 1)
                if i in (10, 12):
                    waits_apart(dve, (s_ch, CHAIN * g + i + 1))
                else:
                    dve.wait_ge(s_ch, CHAIN * g + i + 1)

            def stats(src, g, i0):
                for t in range(4):
                    ins = nc.vector.bn_stats(st2[:, t, :], src[t])
                link(ins, g, i0)
                me, mo = st2[:, :, 1], st2[:, :, 4]
                nc.vector.tensor_tensor(sm2[:, 0, :], me, mo, ALU.add)
                nc.vector.tensor_tensor(sm2[:, 1, :], me, mo, ALU.subtract)
                link(nc.vector.tensor_tensor(sm2[:, 2, :], st2[:, :, 2], st2[:, :, 5], ALU.add), g, i0 + 1)
                nc.vector.tensor_tensor(sm2[:, 3, :], sm2[:, 1, :], sm2[:, 1, :], ALU.mult)
                nc.vector.tensor_scalar(sm2[:, 0, :], sm2[:, 0, :], 0.5, None, ALU.mult)
                eps = ATTN_EPS if i0 == 0 else LN_EPS
                link(nc.vector.tensor_scalar(sm2[:, 2, :], sm2[:, 2, :], 1.0 / D, eps, ALU.mult, ALU.add),
                     g, i0 + 2)
                nc.vector.scalar_tensor_tensor(sm2[:, 4, :], sm2[:, 3, :], 0.25, sm2[:, 2, :], ALU.mult,
                                               ALU.add).then_inc(s_v2, 1)

            def add_expert(m, e):
                dve.wait_ge(s_w2, UNITS * m + FC * (e + 1))
                wait(dve, s_cb, E * m + e)
                dve.wait_ge(s_rt, m + 1)
                if e == 1:
                    dve.wait_ge(s_acc, m + 1)
                for t in range(4):
                    a = xb[:, bass.ds(4 * m + t, 1), :].rearrange("p a d -> p (a d)")
                    ins = nc.vector.scalar_tensor_tensor(a, psum[:, 3 + e % 2, t * P:(t + 1) * P],
                                                         rt[:, t, e:e + 1], a, ALU.mult, ALU.add)
                ins.then_inc(s_cb, 1)

            def slot(g, s):
                if s == 3 and ok(g - 1):
                    add_expert(g - 1, E - 1)
                if ok(g + 1) and s in T_SLOT:
                    c = T_SLOT[s]
                    dve.wait_ge(s_cth, NC * (g + 1) + c + 1)
                    nc.vector.tensor_tensor(cT_lo[:, c % 2, :], psum[:, 5, :], cT_hi[:, c % 2, :],
                                            ALU.subtract).then_inc(s_ctl, 1)
                if ok(g) and s % BY_VECTOR == 0 and s > 0:
                    low(g, s - 1)
                if ok(g - 1) and s == 0:
                    low(g - 1, UNITS - 1)
                if ok(g) and s > 4 and s % FC == 3:
                    add_expert(g, s // FC - 1)
                if ok(g + 1) and s == 18:
                    dve.wait_ge(s_cm, NC * (g + 2))
                    dve.wait_ge(s_bo, g + 2)
                    nc.vector.tensor_tensor(y[:], psum[:, ATTN_OUT(g + 1), :].rearrange("p (t d) -> p t d", t=4),
                                            xnb[:, bass.ds(4 * (g + 1), 4), :], ALU.add).then_inc(s_ao, 1)
                    dve.wait_ge(s_ao, g + 2)
                    stats([y[:, t, :] for t in range(4)], g + 1, 0)
                    for t in range(4):
                        ins = nc.vector.scalar_tensor_tensor(z[:, t, :], y[:, t, :], sm2[:, 0, t:t + 1], gamma_b[:],
                                                             ALU.subtract, ALU.mult)
                    ins.then_inc(s_z, 1)
                if ok(g + 1) and s == 20:
                    dve.wait_ge(s_z, g + 2)
                    dve.wait_ge(s_beta, g + 2)
                    dve.wait_ge(s_r2, 2 * (g + 1) + 1)
                    for t in range(4):
                        a = xb[:, bass.ds(4 * (g + 1) + t, 1), :].rearrange("p a d -> p (a d)")
                        ins = nc.vector.scalar_tensor_tensor(a, z[:, t, :], sm2[:, 5, t:t + 1], a, ALU.mult, ALU.add)
                    ins.then_inc(s_x1, 1)
                if ok(g + 1) and s == 24:
                    waits_apart(dve, (s_x1, g + 2))
                    stats([xb[:, bass.ds(4 * (g + 1) + t, 1), :].rearrange("p a d -> p (a d)")
                           for t in range(4)], g + 1, 3)
                if ok(g + 1) and s == 26:
                    dve.wait_ge(s_r2, 2 * (g + 1) + 2)
                    for t in range(4):
                        a = xb[:, bass.ds(4 * (g + 1) + t, 1), :].rearrange("p a d -> p (a d)")
                        ins = nc.vector.tensor_scalar(x2[:, t, :], a, sm2[:, 0, t:t + 1],
                                                      sm2[:, 5, t:t + 1], ALU.subtract, ALU.mult)
                    ins.then_inc(s_x2, 1)
                if ok(g + 1) and s == X2T_SLOT:
                    dve.wait_ge(s_x2h, g + 2)
                    c = bass.ds((g + 1) * 512, 512)
                    nc.vector.tensor_tensor(xT_lo[:, c], psum[:, 7, :], xT_hi[:, c],
                                            ALU.subtract).then_inc(s_x2l, 1)
                if ok(g + 1) and s == 31:
                    dve.wait_ge(s_lg, g + 2)
                    if isinstance(g, int) and g == -1:
                        dve.wait_ge(s_pv, STEPS * PAIRS)
                    link(nc.vector.tensor_tensor(lg[:], psum[:, 7, 0:4 * E].rearrange("p (t e) -> p t e", t=4),
                                                 br_b[:].unsqueeze(1).to_broadcast([P, 4, E]), ALU.add),
                         g + 1, 6)
                    link(nc.vector.reduce_max(rs[:, 0, :], lg[:], AX.X), g + 1, 7)
                    nc.vector.tensor_tensor(lg2[:], lg[:], rs[:, 0, :].unsqueeze(2).to_broadcast([P, 4, E]),
                                            ALU.subtract).then_inc(s_lgr, 1)
                if ok(g) and s == 3:
                    routing(g)
                if ok(g) and s == B2_SLOT + 1:
                    dve.wait_ge(s_b2, g + 1)
                    dve.wait_ge(s_cb, E * g + 1)
                    a = xb[:, bass.ds(4 * g, 4), :]
                    nc.vector.tensor_tensor(a, psum[:, 7, :].rearrange("p (t d) -> p t d", t=4), a,
                                            ALU.add).then_inc(s_acc, 1)

            def low(m, t):
                dve.wait_ge(s_h32, UNITS * m + t + 1)
                nc.vector.tensor_tensor(h_lo[:, t % 4, :], h32[:, t % 4, :], high_half(h32[:, t % 4, :]),
                                        ALU.subtract).then_inc(s_hlv, 1)

            def routing(g):
                dve.wait_ge(s_le, g + 1)
                link(nc.vector.reduce_sum(rs[:, 1, :], pe_[:], AX.X), g, 8)
                link(nc.vector.reciprocal(rs[:, 2, :], rs[:, 1, :]), g, 9)
                link(nc.vector.tensor_tensor(pr[:], pe_[:], rs[:, 2, :].unsqueeze(2).to_broadcast([P, 4, E]),
                                             ALU.mult), g, 10)
                for t in range(4):
                    ins = nc.vector.max(top[:, t, :], pr[:, t, :])
                link(ins, g, 11)
                link(nc.vector.memset(top[:, :, 2:8], -1.0), g, 12)
                for t in range(4):
                    ins = nc.vector.match_replace(out=rest[:, t, :], in_to_replace=top[:, t, :],
                                                  in_values=pr[:, t, :], imm_value=0.0)
                link(ins, g, 13)
                link(nc.vector.tensor_tensor(wsel[:], pr[:], rest[:], ALU.subtract), g, 14)
                link(nc.vector.reduce_sum(rs[:, 3, :], wsel[:], AX.X), g, 15)
                link(nc.vector.reciprocal(rs[:, 3, :], rs[:, 3, :]), g, 16)
                nc.vector.tensor_tensor(rt[:], wsel[:], rs[:, 3, :].unsqueeze(2).to_broadcast([P, 4, E]),
                                        ALU.mult).then_inc(s_rt, 1)

            return slot

        with nc.Block() as block:
            @block.sync
            def _(sp):
                setup_sync(sp)
                attention_sync(sp)
                experts_sync(sp)

            @block.scalar
            def _(act):
                early, slot = setup_scalar(act), experts_scalar(act)
                attention_scalar(act, early, slot)
                groups(act, slot)

            @block.gpsimd
            def _(pool):
                early, slot = setup_gpsimd(pool), experts_gpsimd(pool)
                attention_gpsimd(pool, early, slot)
                groups(pool, slot)

            @block.tensor
            def _(pe):
                early, slot = setup_tensor(pe), experts_tensor(pe)
                attention_tensor(pe, early, slot)
                groups(pe, slot)

            @block.vector
            def _(dve):
                early, slot = setup_vector(dve), experts_vector(dve)
                attention_vector(dve, early, slot)
                groups(dve, slot)


_INS = ["L0_attn_x", "L0_attn_Wq", "L0_attn_bq", "L0_attn_Wk", "L0_attn_bk", "L0_attn_Wv", "L0_attn_bv", "L0_attn_Wo",
        "L0_attn_bo", "L0_attn_gamma", "L0_attn_beta", "L0_ffn_W1", "L0_ffn_b1", "L0_ffn_W2", "L0_ffn_b2",
        "L0_ffn_Wr", "L0_ffn_br"]


def kernel(**inputs):
    import numpy as np
    import concourse.bacc as bacc
    from concourse.bass_utils import run_bass_kernel_spmd

    nc = bacc.Bacc("TRN2", target_bir_lowering=False, num_devices=1)
    arrays, args = {}, []
    for name in _INS:
        a = np.ascontiguousarray(inputs[name])
        arrays[f"in_{name}"] = a
        args.append(nc.dram_tensor(f"in_{name}", a.shape, mybir.dt.from_np(a.dtype), kind="ExternalInput").ap())
    out = nc.dram_tensor("out_0", inputs["L0_attn_x"].shape, F32, kind="ExternalOutput").ap()
    block_kernel(nc, *args, out)
    r = run_bass_kernel_spmd(nc, [arrays], core_ids=[0])
    return r.results[0]["out_0"]
```
